# Optimizing a Trainium2 kernel written in Bass

```python
import numpy as np
import jax
import jax.numpy as jnp

def _softmax(x, axis=-1):
    return jax.nn.softmax(x, axis=axis)

def _gelu(x):
    return jax.nn.gelu(x, approximate=True)

def _silu(x):
    return jax.nn.silu(x)

def _sigmoid(x):
    return jax.nn.sigmoid(x)

def _layernorm(x, axis=-1, eps=1e-05):
    m = jnp.mean(x, axis=axis, keepdims=True)
    v = jnp.var(x, axis=axis, keepdims=True)
    return (x - m) / jnp.sqrt(v + eps)

def _scatter_add(tgt, idx, src, axis=0):
    return tgt.at[idx].add(src)

def _segment_sum(src, seg, n):
    return jax.ops.segment_sum(src, seg, n)
kernel_name = 'mk_macaron_d1_jaxref_r4_4d6790'

def setup_inputs(seed: int=0):
    np.random.seed(seed)
    _w = jnp.asarray

    def _L0_attn_setup():
        import jax, jax.numpy as jnp
        import numpy as np
        D_MODEL = 512
        N_HEADS = 16
        HEAD_DIM = D_MODEL // N_HEADS
        SCALE_BASE = 128

        def rotate_half(x):
            x1, x2 = jnp.split(x, 2, axis=-1)
            return jnp.concatenate((-x2, x1), axis=-1)

        def rotary_xpos(seq_len, dim, dtype=jnp.float32):
            inv_freq = 1.0 / 10000.0 ** (jnp.arange(0, dim, 2, dtype=jnp.float32) / dim)
            t = jnp.arange(seq_len, dtype=jnp.float32)
            freqs = jnp.einsum('i,j->ij', t, inv_freq)
            freqs = jnp.concatenate((freqs, freqs), axis=-1)
            scale_base = (jnp.arange(0, dim, 2, dtype=jnp.float32) + 0.4 * dim) / (1.4 * dim)
            power = (t - seq_len // 2) / SCALE_BASE
            scale = scale_base[None, :] ** power[:, None]
            scale = jnp.concatenate((scale, scale), axis=-1)
            return (freqs.astype(dtype), scale.astype(dtype))

        def apply_rotary(t, pos, scale):
            return t * jnp.cos(pos) * scale + rotate_half(t) * jnp.sin(pos) * scale
        key = jax.random.key(seed)
        ks = jax.random.split(key, 5)
        B, S = (2, 512)
        hidden_states = jax.random.normal(ks[0], (B, S, D_MODEL), dtype=jnp.float32)
        w_q = jax.random.normal(ks[1], (N_HEADS * HEAD_DIM, D_MODEL), dtype=jnp.float32) * 0.02
        w_kv = jax.random.normal(ks[2], (2 * HEAD_DIM, D_MODEL), dtype=jnp.float32) * 0.02
        w_proj = jax.random.normal(ks[3], (D_MODEL, N_HEADS * HEAD_DIM), dtype=jnp.float32) * 0.02
        b_proj = jax.random.normal(ks[4], (D_MODEL,), dtype=jnp.float32) * 0.02
        return {'hidden_states': hidden_states, 'w_q': w_q, 'w_kv': w_kv, 'w_proj': w_proj, 'b_proj': b_proj}
    _L0_attn_in = _L0_attn_setup()

    def _L0_ffn_setup():
        import jax, jax.numpy as jnp
        import numpy as np

        def _sparsify_2to4(h):
            B, S, I = h.shape
            g = h.reshape(B, S, I // 4, 4)
            a = jnp.abs(g)
            _, idx = jax.lax.top_k(a, 2)
            pos = jnp.arange(4)
            mask = (pos == idx[..., 0:1]) | (pos == idx[..., 1:2])
            return (g * mask.astype(g.dtype)).reshape(B, S, I)
        key = jax.random.key(seed)
        k1, k2, k3, k4 = jax.random.split(key, 4)
        B, S, H, I = (4, 512, 512, 2048)
        x = jax.random.normal(k1, (B, S, H), dtype=jnp.float32)
        w_gate = jax.random.normal(k2, (H, I), dtype=jnp.float32) / np.sqrt(H)
        w_up = jax.random.normal(k3, (H, I), dtype=jnp.float32) / np.sqrt(H)
        w_down = jax.random.normal(k4, (I, H), dtype=jnp.float32) / np.sqrt(I)
        return {'x': x, 'w_gate': w_gate, 'w_up': w_up, 'w_down': w_down}
    _L0_ffn_in = _L0_ffn_setup()
    _d = {'L0_attn_hidden_states': _L0_attn_in['hidden_states'], 'L0_attn_w_q': _L0_attn_in['w_q'], 'L0_attn_w_kv': _L0_attn_in['w_kv'], 'L0_attn_w_proj': _L0_attn_in['w_proj'], 'L0_attn_b_proj': _L0_attn_in['b_proj'], 'L0_ffn_w_gate': _L0_ffn_in['w_gate'], 'L0_ffn_w_up': _L0_ffn_in['w_up'], 'L0_ffn_w_down': _L0_ffn_in['w_down']}
    _x0 = _d['L0_attn_hidden_states']
    _d['L0_attn_hidden_states'] = jax.random.normal(jax.random.fold_in(jax.random.key(seed), 1), (8, 512, 512), dtype=_x0.dtype)
    del _x0
    return _d

def reference(L0_attn_hidden_states, L0_attn_w_q, L0_attn_w_kv, L0_attn_w_proj, L0_attn_b_proj, L0_ffn_w_gate, L0_ffn_w_up, L0_ffn_w_down):

    def _L0_attn_ref(hidden_states, w_q, w_kv, w_proj, b_proj):
        import jax, jax.numpy as jnp
        import numpy as np
        D_MODEL = 512
        N_HEADS = 16
        HEAD_DIM = D_MODEL // N_HEADS
        SCALE_BASE = 128

        def rotate_half(x):
            x1, x2 = jnp.split(x, 2, axis=-1)
            return jnp.concatenate((-x2, x1), axis=-1)

        def rotary_xpos(seq_len, dim, dtype=jnp.float32):
            inv_freq = 1.0 / 10000.0 ** (jnp.arange(0, dim, 2, dtype=jnp.float32) / dim)
            t = jnp.arange(seq_len, dtype=jnp.float32)
            freqs = jnp.einsum('i,j->ij', t, inv_freq)
            freqs = jnp.concatenate((freqs, freqs), axis=-1)
            scale_base = (jnp.arange(0, dim, 2, dtype=jnp.float32) + 0.4 * dim) / (1.4 * dim)
            power = (t - seq_len // 2) / SCALE_BASE
            scale = scale_base[None, :] ** power[:, None]
            scale = jnp.concatenate((scale, scale), axis=-1)
            return (freqs.astype(dtype), scale.astype(dtype))

        def apply_rotary(t, pos, scale):
            return t * jnp.cos(pos) * scale + rotate_half(t) * jnp.sin(pos) * scale
        B, S, _ = hidden_states.shape
        q = hidden_states @ w_q.T
        kv = hidden_states @ w_kv.T
        k, v = jnp.split(kv, 2, axis=-1)
        q = q.reshape(B, S, N_HEADS, HEAD_DIM).transpose(0, 2, 1, 3)
        scale_w = HEAD_DIM ** (-0.5)
        q = q * scale_w
        k = k * scale_w
        pos, xscale = rotary_xpos(S, HEAD_DIM, q.dtype)
        q = apply_rotary(q, pos, xscale)
        k = apply_rotary(k, pos, 1.0 / xscale)
        attn = jnp.einsum('bnih,bjh->bnij', q, k)
        causal = jnp.triu(jnp.ones((S, S), dtype=bool), 1)
        attn = jnp.where(causal, -jnp.finfo(attn.dtype).max, attn)
        attn = jax.nn.softmax(attn, axis=-1)
        out = jnp.einsum('bnij,bjd->bind', attn, v)
        out = out.reshape(B, S, N_HEADS * HEAD_DIM)
        out = out @ w_proj.T + b_proj
        return out

    def _L0_ffn_ref(x, w_gate, w_up, w_down):
        import jax, jax.numpy as jnp
        import numpy as np

        def _sparsify_2to4(h):
            B, S, I = h.shape
            g = h.reshape(B, S, I // 4, 4)
            a = jnp.abs(g)
            _, idx = jax.lax.top_k(a, 2)
            pos = jnp.arange(4)
            mask = (pos == idx[..., 0:1]) | (pos == idx[..., 1:2])
            return (g * mask.astype(g.dtype)).reshape(B, S, I)
        h = jax.nn.silu(jnp.einsum('bsh,hi->bsi', x, w_gate)) * jnp.einsum('bsh,hi->bsi', x, w_up)
        h_sparse = _sparsify_2to4(h)
        return jnp.einsum('bsi,ih->bsh', h_sparse, w_down)
    x = L0_attn_hidden_states
    x = x + 0.5 * _L0_ffn_ref(_layernorm(x, axis=-1), L0_ffn_w_gate, L0_ffn_w_up, L0_ffn_w_down)
    x = x + _L0_attn_ref(_layernorm(x, axis=-1), L0_attn_w_q, L0_attn_w_kv, L0_attn_w_proj, L0_attn_b_proj)
    x = x + 0.5 * _L0_ffn_ref(_layernorm(x, axis=-1), L0_ffn_w_gate, L0_ffn_w_up, L0_ffn_w_down)
    return x

_drawn_inputs = setup_inputs


def setup_inputs(seed=0):
    import zlib

    import numpy as np

    out = dict(_drawn_inputs(seed))
    spreads = {}
    factors = {'L0_attn_w_q': 63.251, 'L0_attn_b_proj': 2.729}
    for name, (base, spread) in spreads.items():
        noise = np.random.default_rng([zlib.crc32(name.encode()), seed]).standard_normal(out[name].shape)
        drawn = base * np.exp(spread * noise) if base else spread * noise
        out[name] = jnp.asarray(drawn.astype(out[name].dtype))
    for name, factor in factors.items():
        out[name] = (out[name] * factor).astype(out[name].dtype)
    return out
```

```python
from contextlib import ExitStack

import concourse.bass as bass
from concourse import mybir

F32 = mybir.dt.float32
F32R = mybir.dt.float32r
BF16 = mybir.dt.bfloat16
ALU = mybir.AluOpType
ACT = mybir.ActivationFunctionType
AX = mybir.AxisListType

P = 128
EPS = 1e-5
MASKED = -3.0e38


def macaron_kernel(nc, x_in, w_gu, w_d, w_q, w_kv, w_p, b_p, rotary, out):
    BATCHES, S, D = x_in.shape
    KD = D // P
    NCH, NR = w_gu.shape[0], w_gu.shape[1]
    TT = S // P
    NB = 2
    GROUPS = BATCHES // NB
    STEPS = NCH * NB
    HD = w_kv.shape[2] // 2
    HEADS = D // HD
    HG = P // HD
    NHG = HEADS // HG
    assert TT == KD == NR == NHG == HG == 4

    x_mid = [nc.dram_tensor(f"x_mid{i}", [BATCHES, S, D], F32, kind="Internal").ap() for i in range(2)]

    def tiles(ap):
        return ap.rearrange("b (t p) d -> b p t d", p=P)

    at = [(nc.sbuf_base + 63) // 64 * 64]

    def place(name, shape, dt):
        size = 1
        for s in shape[1:]:
            size *= s
        size *= 2 if dt == BF16 else 4
        t = nc.alloc_sbuf_tensor_at(name, shape, dt, offset=at[0])
        at[0] += (size + 31) // 32 * 32
        return t

    ident = place("ident", [P, P], F32)
    ident_b = place("ident_b", [P, P], BF16)
    mask_b = place("mask_b", [P, P], BF16)
    halves = place("halves", [P, TT], F32)
    x_sb = place("x_sb", [P, 2, NB * TT, D], F32)
    xnt_h = place("xnt_h", [P, NB, KD, S], F32R)
    xnt_l = place("xnt_l", [P, NB, KD, S], F32R)
    xn = place("xn", [P, 2, D], F32)
    stats = place("stats", [P, TT, 6], F32)
    meanvar = place("meanvar", [P, TT, 2], F32)
    var_eps = place("var_eps", [P, TT], F32)
    rstd = place("rstd", [P, TT], F32)
    shared_end = at[0]

    wgu_h = place("wgu_h", [P, NR, 2, KD, P], F32R)
    wgu_l = place("wgu_l", [P, NR, 2, KD, P], F32R)
    wd_h = place("wd_h", [P, NR, D], F32R)
    wd_l = place("wd_l", [P, NR, D], F32R)
    raw_gu = place("raw_gu", [P, NR, 2, KD, P], F32)
    raw_d = place("raw_d", [P, NR, D], F32)
    sg = place("sg", [P, 2, S], F32)
    h = place("h", [P, NR, S], F32)
    mag = place("mag", [P, NR, S], F32)
    pmax = place("pmax", [P, 2, S], F32)
    first = place("first", [P, 2, S], BF16)
    kept_k = place("kept_k", [P, 2, S], BF16)
    kept_a = place("kept_a", [P, S], BF16)
    ksum = place("ksum", [P, 2, S], BF16)
    kdif = place("kdif", [P, 2, S], BF16)
    hs_h = place("hs_h", [P, NB, NR, S], F32R)
    hs_l = place("hs_l", [P, NB, NR, S], F32R)
    ffn_end = at[0]

    at[0] = shared_end
    wq_h = place("wq_h", [P, KD, D], F32R)
    wq_l = place("wq_l", [P, KD, D], F32R)
    wp_h = place("wp_h", [P, KD, D], F32R)
    wp_l = place("wp_l", [P, KD, D], F32R)
    wkv_h = place("wkv_h", [P, KD, 2 * HD], F32R)
    wkv_l = place("wkv_l", [P, KD, 2 * HD], F32R)
    rot = place("rot", [P, TT, 4, HD], F32)
    bias = place("bias", [P, D], F32)
    kvt = place("kvt", [2 * HD, S], F32)
    krot = place("krot", [P, 2, TT, HD], F32)
    kstack = place("kstack", [P, TT, P], F32)
    kt = place("kt", [P, S], F32R)
    VW = 2 * (P - HD) + HD
    v_h = place("v_h", [P, TT, VW], F32R)
    v_l = place("v_l", [P, TT, VW], F32R)
    qrot = place("qrot", [P, TT, D], F32)
    qstack = place("qstack", [P, TT, HG, P], F32)
    qt = place("qt", [P, HG, S], F32R)
    nmax = place("nmax", [P, 2, TT], F32)
    sums = place("sums", [P, 2, HG, TT], F32)
    rsum = place("rsum", [P, HG, TT], F32)
    probs = place("probs", [P, 2, TT, S], F32)
    pt_h = place("pt_h", [P, 2, TT, S], F32R)
    pt_l = place("pt_l", [P, 2, TT, S], F32R)
    rwide = place("rwide", [P, TT, HG, HD], F32)
    att_end = at[0]
    assert max(ffn_end, att_end) <= nc.sbuf_usable_end, (ffn_end, att_end, nc.sbuf_usable_end)
    raw_q, raw_p = probs[:, 0], probs[:, 1]
    raw_kv = qrot[:, 0, 0:KD * 2 * HD].rearrange("p (k n) -> p k n", k=KD)
    att_h, att_l = xnt_h[:, 1], xnt_l[:, 1]
    rt, att, qtmp = x_sb[:, 0, TT], x_sb[:, 0, TT + 1], x_sb[:, 0, TT + 2]

    with ExitStack() as ctx:
        def sem(name):
            return ctx.enter_context(nc.semaphore(name))

        def sems(name, n):
            return [sem(f"{name}{i}") for i in range(n)]

        bank = [ctx.enter_context(nc.psum_tensor(f"bank{i}", [P, 512], F32)) for i in range(8)]

        const_pool = sem("const_pool")
        passed_vector, passed_gpsimd, passed_tensor = sem("passed_vector"), sem("passed_gpsimd"), sem("passed_tensor")
        x_loaded = sems("x_loaded", NB)
        x_stored = sem("x_stored")
        gu_loaded = sems("gu_loaded", NR)
        d_loaded = sems("d_loaded", NR)
        ln_stat = sem("ln_stat")
        rstd_step = sem("rstd_step")
        xn_done = sem("xn_done")
        xn_turned = sem("xn_turned")
        xnt_h_done = sem("xnt_h_done")
        xnt_done = sem("xnt_done")
        wgu_h_done = sem("wgu_h_done")
        wgu_done = sem("wgu_done")
        wd_h_done = sem("wd_h_done")
        wd_done = sem("wd_done")
        gate_done = sem("gate_done")
        up_done = sem("up_done")
        silu_done = sem("silu_done")
        h_done = sem("h_done")
        mag_done = sem("mag_done")
        rank_step = sem("rank_step")
        pruned = sem("pruned")
        hs_h_done = sem("hs_h_done")
        hs_done = sem("hs_done")
        down_done = sem("down_done")
        added = sem("added")
        RANK = 8
        aw_loaded = sems("aw_loaded", 5)
        aw_h_done = sem("aw_h_done")
        aw_done = sem("aw_done")
        pad_done = sem("pad_done")
        ax_loaded = sem("ax_loaded")
        kv_done = sem("kv_done")
        kvt_done = sem("kvt_done")
        kv_turned = sem("kv_turned")
        k_step = sem("k_step")
        v_h_done = sem("v_h_done")
        v_done = sem("v_done")
        k_turned = sem("k_turned")
        kt_done = sem("kt_done")
        q_done = sem("q_done")
        q_step = sem("q_step")
        stack_h = sem("stack_h")
        stack_done = sem("stack_done")
        stack_turned = sem("stack_turned")
        qt_done = sem("qt_done")
        score_done = sem("score_done")
        max_done = sem("max_done")
        exp_done = sem("exp_done")
        p_turned = sem("p_turned")
        pt_h_done = sem("pt_h_done")
        pt_done = sem("pt_done")
        pv_done = sem("pv_done")
        rsum_done = sem("rsum_done")
        rwide_done = sem("rwide_done")
        r_turned = sem("r_turned")
        rt_done = sem("rt_done")
        att_done = sem("att_done")
        att_h_done = sem("att_h_done")
        att_l_done = sem("att_l_done")
        proj_done = sem("proj_done")
        x_biased = sem("x_biased")
        x_summed = sem("x_summed")
        ax_stored = sem("ax_stored")

        def passed(engine, mark):
            engine.sem_inc(mark, 1)

        def ln_vector(v, m, xt, slot, wait_x):
            wait_x(v)
            for t in range(TT):
                v.bn_stats(stats[:, t], xt(t)).then_inc(ln_stat, 1)
            v.wait_ge(ln_stat, m * 2 * TT + TT)
            passed(v, passed_vector)
            for t in range(TT):
                v.bn_aggr(meanvar[:, t], stats[:, t]).then_inc(ln_stat, 1)
            v.wait_ge(ln_stat, m * 2 * TT + 2 * TT)
            v.wait_ge(rstd_step, m * 2 + 2)
            for t in range(TT):
                v.wait_ge(xn_turned, m * TT + t + 1)
                v.tensor_scalar(xn[:, t % 2], xt(t), meanvar[:, t, 0:1], rstd[:, t:t + 1],
                                ALU.subtract, ALU.mult).then_inc(xn_done, 1)
                if t >= 1:
                    ln_low(v, m, t - 1, slot)
            ln_low(v, m, TT - 1, slot)

        def ln_low(v, m, t, slot):
            tok = slice(t * P, (t + 1) * P)
            v.wait_ge(xnt_h_done, m * TT + t + 1)
            v.tensor_tensor(xnt_l[:, slot, :, tok], bank[4 + t][:, :].rearrange("p (k n) -> p k n", k=KD),
                            xnt_h[:, slot, :, tok].bitcast(F32), ALU.subtract).then_inc(xnt_done, 1)

        def ln_scalar(a, m, slot):
            for t in range(TT):
                a.wait_ge(xn_turned, m * TT + t + 3)
                a.copy(xnt_h[:, slot, :, t * P:(t + 1) * P],
                       bank[4 + t][:, :].rearrange("p (k n) -> p k n", k=KD)).then_inc(xnt_h_done, 1)

        def ln_tensor(pe, m, bank_free):
            for t in range(TT):
                bank_free(t)
                pe.wait_ge(xn_done, m * TT + t + 1)
                for k in range(KD):
                    last = pe.transpose(bank[4 + t][:, k * P:(k + 1) * P], xn[:, t % 2, k * P:(k + 1) * P],
                                        ident[:, :])
                last.then_inc(xn_turned, 1)

        def ln_gpsimd(g, m):
            g.wait_ge(ln_stat, m * 2 * TT + 2 * TT)
            passed(g, passed_gpsimd)
            g.tensor_scalar(var_eps[:, :], meanvar[:, :, 1], EPS, None, ALU.add).then_inc(rstd_step, 1)
            g.wait_ge(rstd_step, m * 2 + 1)
            g.tensor_tensor(rstd[:, :], var_eps[:, :], halves[:, :], ALU.pow).then_inc(rstd_step, 1)

        def ffn_phase(phase, src, dst, m0):
            n0 = phase * GROUPS * STEPS
            c0 = phase * GROUPS * NCH
            src_t, dst_t = tiles(src), tiles(dst)
            block = nc.Block()

            def body(block):
                @block.sync
                def _(sp):
                    def load_gu(load, c):
                        for r in range(NR):
                            if isinstance(load, int):
                                if load > 0:
                                    sp.wait_ge(wgu_done, load * NR)
                            else:
                                sp.wait_ge(wgu_done, (load - 1) * NR + r + 1)
                            sp.dma_start(raw_gu[:, r], w_gu[c, r]).then_inc(gu_loaded[r], 16)

                    def load_d(c):
                        for r in range(NR):
                            sp.dma_start(raw_d[:, r], w_d[c, r]).then_inc(d_loaded[r], 16)

                    def load_x(g, par):
                        for b in range(NB):
                            sp.dma_start(x_sb[:, par, b * TT:(b + 1) * TT], src_t[g * NB + b]).then_inc(x_loaded[b], 16)

                    def store_x(g):
                        for b in range(NB):
                            sp.wait_ge(added, (n0 + g * STEPS + STEPS - NB + b) * TT + 2 * TT)
                            sp.dma_start(dst_t[g * NB + b], x_sb[:, g % 2, b * TT:(b + 1) * TT]).then_inc(x_stored, 16)

                    def group_weights(g):
                        with sp.Fori(0, NCH) as c:
                            chunk = g * NCH + c
                            load_gu(chunk + (c0 + phase + 1), (c + 1) % NCH)
                            for r in range(NR):
                                sp.wait_ge(wd_done, (chunk + c0) * NR + r + 1)
                                sp.dma_start(raw_d[:, r], w_d[(c + 1) % NCH, r]).then_inc(d_loaded[r], 16)

                    load_x(0, 0)
                    load_gu(c0 + phase, 0)
                    load_d(0)
                    for b in range(NB):
                        sp.wait_ge(x_loaded[b], (phase * GROUPS + 1) * 16)
                    load_x(1, 1)
                    group_weights(0)
                    store_x(0)
                    with sp.Fori(1, GROUPS - 1) as g:
                        sp.wait_ge(x_stored, (g + phase * GROUPS) * NB * 16)
                        load_x(g + 1, (g + 1) % 2)
                        group_weights(g)
                        store_x(g)
                    group_weights(GROUPS - 1)
                    store_x(GROUPS - 1)
                    sp.wait_ge(x_stored, (phase + 1) * GROUPS * NB * 16)
                    for r in range(NR):
                        sp.wait_ge(d_loaded[r], (c0 + phase + GROUPS * NCH + 1) * 16)

                @block.gpsimd
                def _(g):
                    with g.Fori(0, GROUPS * NB) as m:
                        ln_gpsimd(g, m + m0)

                @block.tensor
                def _(pe):
                    def gate_up(n, b, cw):
                        for r in range(NR):
                            if b == 0:
                                pe.wait_ge(wgu_done, cw * NR + r + 1)
                            for kind, done, free, banks in ((0, gate_done, silu_done, 0), (1, up_done, h_done, 2)):
                                pe.wait_ge(free, n * NR + r + 1)
                                ps = bank[banks + r % 2][:, :]
                                i = 0
                                for k in range(KD):
                                    for w, xs in ((wgu_h, xnt_h), (wgu_h, xnt_l), (wgu_l, xnt_h)):
                                        last = pe.matmul(ps, w[:, r, kind, k], xs[:, b, k], start=(i == 0),
                                                         stop=(i == 3 * KD - 1))
                                        i += 1
                                last.then_inc(done, 1)

                    def down(n, b, chunk):
                        pe.wait_ge(hs_done, n * NR + 2 * NR)
                        if b == 0:
                            pe.wait_ge(wd_done, chunk * NR + NR)
                        for t in range(TT):
                            pe.wait_ge(added, n * TT + t + 1)
                            tok = slice(t * P, (t + 1) * P)
                            i = 0
                            for r in range(NR):
                                for hs, w in ((hs_h, wd_h), (hs_h, wd_l), (hs_l, wd_h)):
                                    last = pe.matmul(bank[4 + t][:, :], hs[:, b, r, tok], w[:, r], start=(i == 0),
                                                     stop=(i == 3 * NR - 1))
                                    i += 1
                            last.then_inc(down_done, 1)

                    if phase == 0:
                        pe.sem_inc(xn_turned, 2)
                        pe.sem_inc(down_done, TT)
                        pe.wait_ge(const_pool, 7)
                    with pe.Fori(0, GROUPS) as g:
                        n = g * STEPS + n0
                        m = g * NB + m0
                        ln_tensor(pe, m, lambda t: pe.wait_ge(added, n * TT + t + 1))
                        ln_tensor(pe, m + 1, lambda t: pe.wait_ge(xnt_done, m * TT + t + 1))
                        pe.wait_ge(xnt_done, m * TT + 2 * TT)
                        cw = g * NCH + (c0 + phase)
                        chunk = g * NCH + c0
                        gate_up(n, 0, cw)
                        gate_up(n + 1, 1, cw)
                        down(n, 0, chunk)
                        with pe.Fori(1, NCH) as c:
                            nn = n + c * NB
                            gate_up(nn, 0, cw + c)
                            down(nn - 1, 1, chunk + c - 1)
                            gate_up(nn + 1, 1, cw + c)
                            down(nn, 0, chunk + c)
                        down(n + STEPS - 1, 1, chunk + NCH - 1)

                @block.scalar
                def _(a):
                    def cut_gu(load, r):
                        a.wait_ge(gu_loaded[r], load * 16 + 16)
                        a.copy(wgu_h[:, r], raw_gu[:, r]).then_inc(wgu_h_done, 1)

                    def step(n, b, chunk, load):
                        for r in range(NR):
                            a.wait_ge(gate_done, n * NR + r + 1)
                            a.wait_ge(h_done, n * NR + r + 1)
                            a.activation(sg[:, r % 2], bank[r % 2][:, :], ACT.Silu).then_inc(silu_done, 1)
                            if b == 1:
                                if r == 0:
                                    a.wait_ge(down_done, n * TT)
                                a.wait_ge(d_loaded[r], (chunk + phase) * 16 + 16)
                                a.copy(wd_h[:, r], raw_d[:, r]).then_inc(wd_h_done, 1)
                                if r >= 1:
                                    cut_gu(load, r - 1)
                            a.wait_ge(h_done, n * NR + r + 3)
                            a.activation(mag[:, r], h[:, r], ACT.Abs).then_inc(mag_done, 1)
                        if b == 1:
                            a.wait_ge(up_done, n * NR + NR)
                            cut_gu(load, NR - 1)
                        for r in range(NR):
                            a.wait_ge(pruned, n * NR + r + 1)
                            a.copy(hs_h[:, b, r], h[:, r]).then_inc(hs_h_done, 1)

                    if phase == 0:
                        a.sem_inc(silu_done, 2)
                    for r in range(NR):
                        cut_gu(c0 + phase, r)
                    with a.Fori(0, GROUPS) as g:
                        ln_scalar(a, g * NB + m0, 0)
                        ln_scalar(a, g * NB + (m0 + 1), 1)
                        with a.Fori(0, NCH) as c:
                            n = g * STEPS + c * NB + n0
                            chunk = g * NCH + c + c0
                            step(n, 0, chunk, None)
                            step(n + 1, 1, chunk, chunk + (phase + 1))

                @block.vector
                def _(v):
                    def cut_gu(load, r):
                        v.wait_ge(wgu_h_done, load * NR + r + 1)
                        v.tensor_tensor(wgu_l[:, r], raw_gu[:, r], wgu_h[:, r].bitcast(F32),
                                        ALU.subtract).then_inc(wgu_done, 1)

                    def add_down(n, b, par):
                        for t in range(TT):
                            v.wait_ge(down_done, n * TT + t + 1 + TT)
                            x = x_sb[:, par, b * TT + t]
                            v.scalar_tensor_tensor(out=x, in0=bank[4 + t][:, :], scalar=0.5, in1=x, op0=ALU.mult,
                                                   op1=ALU.add).then_inc(added, 1)

                    def step(n, b, chunk, load, before, par):
                        v.wait_ge(hs_done, n * NR + NR)
                        for r in range(NR):
                            v.wait_ge(up_done, n * NR + r + 1)
                            v.wait_ge(silu_done, n * NR + r + 3)
                            v.tensor_tensor(h[:, r], bank[2 + r % 2][:, :], sg[:, r % 2], ALU.mult).then_inc(h_done, 1)
                            if b == 1:
                                v.wait_ge(wd_h_done, chunk * NR + r + 1)
                                v.tensor_tensor(wd_l[:, r], raw_d[:, r], wd_h[:, r].bitcast(F32),
                                                ALU.subtract).then_inc(wd_done, 1)
                                if r >= 1:
                                    cut_gu(load, r - 1)
                        if b == 1:
                            cut_gu(load, NR - 1)
                        pair = mag[:, :, :].rearrange("p (a e) s -> p a e s", e=2)
                        base = n * RANK
                        v.wait_ge(mag_done, n * NR + NR)
                        v.tensor_tensor(first[:, :, :], pair[:, :, 0], pair[:, :, 1], ALU.is_ge).then_inc(rank_step, 1)
                        v.tensor_tensor(pmax[:, :, :], pair[:, :, 0], pair[:, :, 1], ALU.max).then_inc(rank_step, 1)
                        v.tensor_tensor(pair[:, :, 0], pair[:, :, 0], pair[:, :, 1], ALU.min).then_inc(rank_step, 1)
                        v.wait_ge(rank_step, base + 3)
                        v.tensor_tensor(kept_k[:, 0], mag[:, 0], pmax[:, 1], ALU.is_ge).then_inc(rank_step, 1)
                        v.tensor_tensor(kept_k[:, 1], pmax[:, 0], mag[:, 2], ALU.is_ge).then_inc(rank_step, 1)
                        v.wait_ge(rank_step, base + 5)
                        v.tensor_tensor(kept_a[:, :], kept_k[:, 0], kept_k[:, 1], ALU.add).then_inc(rank_step, 1)
                        v.wait_ge(rank_step, base + 6)
                        wide = kept_a[:, :].unsqueeze(1).to_broadcast([P, 2, S])
                        v.tensor_tensor(ksum[:, :, :], wide, first[:, :, :], ALU.add).then_inc(rank_step, 1)
                        v.tensor_tensor(kdif[:, :, :], wide, first[:, :, :], ALU.subtract).then_inc(rank_step, 1)
                        v.wait_ge(rank_step, base + 8)
                        rules = ((ksum[:, 0], 2.0, ALU.is_ge), (kdif[:, 0], 1.0, ALU.is_ge),
                                 (kdif[:, 1], 0.0, ALU.is_le), (ksum[:, 1], 1.0, ALU.is_le))
                        for r, (count, least, op) in enumerate(rules):
                            v.scalar_tensor_tensor(out=h[:, r], in0=count, scalar=least, in1=h[:, r], op0=op,
                                                   op1=ALU.mult).then_inc(pruned, 1)
                        if before:
                            add_down(n - 1, 1 - b, par)
                        for r in range(NR):
                            v.wait_ge(hs_h_done, n * NR + r + 1)
                            v.tensor_tensor(hs_l[:, b, r], h[:, r], hs_h[:, b, r].bitcast(F32),
                                            ALU.subtract).then_inc(hs_done, 1)

                    if phase == 0:
                        v.sem_inc(h_done, 2)
                        v.sem_inc(hs_done, NR)
                        v.sem_inc(added, TT)
                    for r in range(NR):
                        cut_gu(c0 + phase, r)
                    with v.Fori(0, GROUPS) as g:
                        par = g % 2
                        for b in range(NB):
                            ln_vector(v, g * NB + (m0 + b), lambda t: x_sb[:, par, b * TT + t], b,
                                      lambda v: v.wait_ge(x_loaded[b], (g + phase * GROUPS) * 16 + 16))
                        n = g * STEPS + n0
                        chunk = g * NCH + c0
                        step(n, 0, chunk, None, False, par)
                        step(n + 1, 1, chunk, chunk + (phase + 1), True, par)
                        with v.Fori(1, NCH) as c:
                            step(n + c * NB, 0, chunk + c, None, True, par)
                            step(n + c * NB + 1, 1, chunk + c, chunk + c + (phase + 1), True, par)
                        add_down(n + STEPS - 1, 1, par)

            with block as blk:
                body(blk)

        def attention_phase(src, dst, m0):
            src_t, dst_t = tiles(src), tiles(dst)
            NT = HEADS * TT
            SCORES, TURNS, OUTS, SPARE = 0, 3, 5, 7
            KSTEP, QSTEP = 6, 4
            HALF = HD // 2
            meets = [(j * P if j < TT - 1 else (TT - 2) * P) for j in range(TT)]

            def width(i):
                return (i + 1) * P

            def heads_of(ap):
                return ap.rearrange("p (h d) -> p h d", d=HD)

            with nc.Block() as blk:
                @blk.sync
                def _(sp):
                    sp.dma_start(raw_kv, w_kv).then_inc(aw_loaded[0], 16)
                    sp.dma_start(x_sb[:, 0, 0:TT], src_t[0]).then_inc(ax_loaded, 16)
                    sp.dma_start(raw_q, w_q).then_inc(aw_loaded[1], 16)
                    sp.dma_start(rot[:, :, :, :], rotary).then_inc(aw_loaded[2], 16)
                    sp.dma_start(raw_p, w_p).then_inc(aw_loaded[3], 16)
                    sp.dma_start(bias[:, :], b_p.to_broadcast([P, D])).then_inc(aw_loaded[4], 16)
                    sp.wait_ge(ax_loaded, 16)
                    sp.dma_start(x_sb[:, 1, 0:TT], src_t[1]).then_inc(ax_loaded, 16)

                    def store(B, par):
                        for t in range(TT):
                            sp.wait_ge(x_summed, B * TT + t + 1 + TT)
                            sp.dma_start(dst_t[B, :, t], x_sb[:, par, t]).then_inc(ax_stored, 16)

                    with sp.Fori(0, BATCHES - 2) as B:
                        store(B, B % 2)
                        sp.wait_ge(ax_stored, (B * TT + TT) * 16)
                        sp.wait_ge(ax_loaded, (B + 2) * 16)
                        sp.dma_start(x_sb[:, B % 2, 0:TT], src_t[B + 2]).then_inc(ax_loaded, 16)
                    for B in range(BATCHES - 2, BATCHES):
                        store(B, B % 2)
                    sp.wait_ge(ax_stored, BATCHES * TT * 16)

                def stack_head(g, B, w):
                    g.wait_ge(stack_turned, B * HEADS + w + 1)
                    passed(g, passed_gpsimd)
                    slot = qstack[:, :, w % HG].rearrange("p t (e c d) -> p t e c d", e=2, c=2)
                    q = qrot[:, :, w * HD:(w + 1) * HD].unsqueeze(2).to_broadcast([P, TT, 2, HD])
                    g.tensor_copy(slot[:, :, :, 0].bitcast(F32R), q).then_inc(stack_h, 1)
                    g.wait_ge(stack_h, B * HEADS + w + 1)
                    g.tensor_tensor(slot[:, :, :, 1], q, slot[:, :, :, 0], ALU.subtract).then_inc(stack_done, 1)

                @blk.gpsimd
                def _(g):
                    g.sem_inc(stack_done, HEADS)
                    for t in (v_h, v_l):
                        g.memset(t[:, :, :].bitcast(F32), 0.0).then_inc(pad_done, 1)
                    for t in (pt_h, pt_l):
                        g.memset(t[:, :, TT - 1, meets[-1]:(TT - 1) * P].bitcast(F32), 0.0).then_inc(pad_done, 1)
                    with g.Fori(0, BATCHES) as B:
                        ln_gpsimd(g, B + m0)
                        for w in range(HEADS):
                            if w == 0:
                                g.wait_ge(q_step, B * QSTEP * TT + QSTEP * TT)
                            stack_head(g, B, w)

                @blk.tensor
                def _(pe):
                    pe.sem_inc(stack_turned, HG)

                    def project(ps, w_hi, w_lo, rows, x_is_moving, t=None):
                        i = 0
                        for k in range(KD):
                            for a, b in ((w_hi, xnt_h), (w_lo, xnt_h), (w_hi, xnt_l)):
                                if x_is_moving:
                                    last = pe.matmul(ps, a[:, k], b[:, 0, k], start=(i == 0), stop=(i == 3 * KD - 1))
                                else:
                                    last = pe.matmul(ps, b[:, 0, k, t * P:(t + 1) * P], a[:, k], start=(i == 0),
                                                     stop=(i == 3 * KD - 1))
                                i += 1
                        return last

                    def spare_free(B, uses):
                        if uses and uses[-1][0] == "q":
                            pe.wait_ge(qt_done, B * HEADS + uses[-1][1] + 1)
                        elif uses:
                            pe.wait_ge(rt_done, B * NHG + uses[-1][1] + 1)

                    def turn_stack(B, w, uses):
                        pe.wait_ge(stack_done, B * HEADS + w + 1 + HEADS)
                        spare_free(B, uses)
                        for t in range(TT):
                            last = pe.transpose(bank[SPARE][:, t * P:(t + 1) * P], qstack[:, t, w % HG], ident[:, :])
                        last.then_inc(stack_turned, 1)
                        uses.append(("q", w))

                    def turn_sums(B, hg, uses):
                        pe.wait_ge(rwide_done, B * NHG + hg + 1)
                        spare_free(B, uses)
                        for t in range(TT):
                            last = pe.transpose(bank[SPARE][:, t * P:(t + 1) * P],
                                                rwide[:, t].rearrange("p h d -> p (h d)"), ident[:, :])
                        last.then_inc(r_turned, 1)
                        uses.append(("r", hg))

                    def scores(B, u, i):
                        e = u * TT + i
                        if e >= 3:
                            pe.wait_ge(exp_done, B * NT + e - 2)
                        if i == 0:
                            pe.wait_ge(qt_done, B * HEADS + u + 1)
                        ps = bank[SCORES + e % 3]
                        n = max(width(i), 2 * P)
                        pe.matmul(ps[:, 0:n], qt[:, u % HG, i * P:(i + 1) * P], kt[:, 0:n], start=True, stop=False)
                        pe.matmul(ps[:, i * P:width(i)], ident_b[:, :], mask_b[:, :], start=False,
                                  stop=True).then_inc(score_done, 1)

                    def turn_probs(B, u, i):
                        e = u * TT + i
                        pe.wait_ge(exp_done, B * NT + e + 1)
                        if e >= 2:
                            pe.wait_ge(pt_done, B * NT + e - 1)
                        for j in range(i + 1):
                            last = pe.transpose(bank[TURNS + e % 2][:, j * P:(j + 1) * P],
                                                probs[:, u % 2, i, j * P:(j + 1) * P], ident[:, :])
                        last.then_inc(p_turned, 1)

                    def weigh(B, u, j):
                        hg, s = u // HG, u % HG
                        if j == 0:
                            pe.wait_ge(pt_done, B * NT + u * TT + TT)
                            if s == 0 and hg >= 2:
                                pe.wait_ge(att_done, B * NHG + hg - 1)
                        window = slice((HG - 1 - s) * HD, (HG - 1 - s) * HD + P)
                        a = meets[j]
                        for i, (v, pt) in enumerate(((v_h, pt_h), (v_l, pt_h), (v_h, pt_l))):
                            last = pe.matmul(bank[OUTS + hg % 2][:, a:S], v[:, j, window], pt[:, u % 2, j, a:S],
                                             start=(s == 0 and j == 0 and i == 0),
                                             stop=(s == HG - 1 and j == TT - 1 and i == 2))
                        if j == TT - 1:
                            last.then_inc(pv_done, 1)

                    with pe.Fori(0, BATCHES) as B:
                        m = B + m0
                        uses = []
                        ln_tensor(pe, m, lambda t: pe.wait_ge(x_summed, B * TT + TT) if t == 0 else None)
                        pe.wait_ge(xnt_done, m * TT + TT)
                        pe.wait_ge(aw_done, 2)
                        project(bank[0][0:2 * HD, :], wkv_h, wkv_l, 2 * HD, True).then_inc(kv_done, 1)
                        for t in range(TT):
                            project(bank[4 + t][:, :], wq_h, wq_l, P, False, t).then_inc(q_done, 1)
                            if t == 0:
                                pe.wait_ge(kvt_done, B + 1)
                                passed(pe, passed_tensor)
                                for tt in range(TT):
                                    last = pe.transpose(bank[1][:, tt * 2 * HD:(tt + 1) * 2 * HD],
                                                        kvt[:, tt * P:(tt + 1) * P], ident[0:2 * HD, 0:2 * HD])
                                last.then_inc(kv_turned, 1)
                        pe.wait_ge(k_step, B * KSTEP + KSTEP)
                        for t in range(TT):
                            last = pe.transpose(bank[2][:, t * P:(t + 1) * P], kstack[:, t], ident[:, :])
                        last.then_inc(k_turned, 1)
                        pe.wait_ge(q_step, B * QSTEP * TT + QSTEP * TT)
                        turn_stack(B, 0, uses)
                        turn_stack(B, 1, uses)
                        pe.wait_ge(kt_done, B + 1)
                        pe.wait_ge(v_done, B + 1)
                        for u in range(HEADS + 2):
                            for i in range(TT):
                                if u < HEADS:
                                    scores(B, u, i)
                                if 1 <= u <= HEADS:
                                    turn_probs(B, u - 1, i)
                                if u >= 2:
                                    weigh(B, u - 2, i)
                            if u + 2 < HEADS:
                                turn_stack(B, u + 2, uses)
                            if u >= 2 and (u - 2) % HG == HG - 1:
                                turn_sums(B, (u - 2) // HG, uses)
                        pe.wait_ge(att_l_done, B * NHG + NHG)
                        pe.wait_ge(aw_done, 3)
                        for t in range(TT):
                            i = 0
                            for k in range(KD):
                                for a, w in ((att_h, wp_h), (att_h, wp_l), (att_l, wp_h)):
                                    last = pe.matmul(bank[t][:, :], a[:, k, t * P:(t + 1) * P], w[:, k],
                                                     start=(i == 0), stop=(i == 3 * KD - 1))
                                    i += 1
                            last.then_inc(proj_done, 1)

                @blk.scalar
                def _(a):
                    for i, (ld, hi, raw) in enumerate(((0, wkv_h, raw_kv), (1, wq_h, raw_q), (3, wp_h, raw_p))):
                        a.wait_ge(aw_loaded[ld], 16)
                        a.copy(hi[:, :, :], raw).then_inc(aw_h_done, 1)
                    with a.Fori(0, BATCHES) as B:
                        ln_scalar(a, B + m0, 0)
                        a.wait_ge(kv_done, B + 1)
                        a.copy(kvt[:, :], bank[0][0:2 * HD, :]).then_inc(kvt_done, 1)
                        a.wait_ge(k_step, B * KSTEP + 3)
                        a.wait_ge(pad_done, 4)
                        kv = bank[1][:, 0:TT * 2 * HD].rearrange("p (t c d) -> p t c d", t=TT, c=2)
                        a.copy(v_h[:, :, P - HD:P], kv[:, :, 1]).then_inc(v_h_done, 1)
                        a.wait_ge(k_turned, B + 1)
                        a.copy(kt[:, :], bank[2][:, :]).then_inc(kt_done, 1)

                        def queries(w):
                            a.wait_ge(stack_turned, B * HEADS + w + 1 + HG)
                            a.copy(qt[:, w % HG], bank[SPARE][:, :]).then_inc(qt_done, 1)

                        def cast_output(hg):
                            a.wait_ge(att_done, B * NHG + hg + 1)
                            a.copy(att_h[:, hg], att).then_inc(att_h_done, 1)

                        queries(0)
                        queries(1)
                        for u in range(HEADS + 2):
                            ended = u >= 3 and (u - 3) % HG == HG - 1
                            for i in range(TT):
                                if u < HEADS:
                                    e = u * TT + i
                                    a.wait_ge(max_done, B * NT + e + 1)
                                    a.activation(probs[:, u % 2, i, 0:width(i)], bank[SCORES + e % 3][:, 0:width(i)], ACT.Exp,
                                                 bias=nmax[:, u % 2, i:i + 1],
                                                 accum_out=sums[:, (u // HG) % 2, u % HG, i:i + 1]).then_inc(exp_done, 1)
                                if i == 0 and ended:
                                    cast_output((u - 3) // HG)
                                if 1 <= u <= HEADS:
                                    e = (u - 1) * TT + i
                                    a.wait_ge(p_turned, B * NT + e + 1)
                                    a.copy(pt_h[:, (u - 1) % 2, 0:i + 1, i * P:(i + 1) * P],
                                           bank[TURNS + e % 2][:, 0:width(i)].rearrange("p (j n) -> p j n", n=P)).then_inc(pt_h_done, 1)
                            if u + 2 < HEADS:
                                queries(u + 2)
                            if u >= 2 and (u - 2) % HG == HG - 1:
                                a.wait_ge(r_turned, B * NHG + (u - 2) // HG + 1)
                                a.copy(rt, bank[SPARE][:, :]).then_inc(rt_done, 1)
                        cast_output(NHG - 1)

                @blk.vector
                def _(v):
                    v.sem_inc(x_summed, TT)
                    for i, (hi, lo, raw) in enumerate(((wkv_h, wkv_l, raw_kv), (wq_h, wq_l, raw_q), (wp_h, wp_l, raw_p))):
                        v.wait_ge(aw_h_done, i + 1)
                        v.tensor_tensor(lo[:, :, :], raw, hi[:, :, :].bitcast(F32), ALU.subtract).then_inc(aw_done, 1)
                    v.wait_ge(aw_done, 3)
                    v.wait_ge(aw_loaded[2], 16)
                    v.wait_ge(aw_loaded[4], 16)

                    def rotate(x, dst, tmp, cos, sin, step, base, last):
                        v.tensor_tensor(dst, x, cos, ALU.mult).then_inc(step, 1)
                        v.tensor_tensor(tmp[:, :, 0:HALF], x[:, :, HALF:HD], sin[:, :, 0:HALF], ALU.mult).then_inc(step, 1)
                        v.tensor_tensor(tmp[:, :, HALF:HD], x[:, :, 0:HALF], sin[:, :, HALF:HD], ALU.mult).then_inc(step, 1)
                        v.wait_ge(step, base + 3)
                        v.tensor_tensor(dst, dst, tmp, ALU.add).then_inc(step, 1)
                        if last:
                            v.wait_ge(step, base + 4)

                    with v.Fori(0, BATCHES) as B:
                        m = B + m0
                        par = B % 2
                        ln_vector(v, m, lambda t: x_sb[:, par, t], 0, lambda v: v.wait_ge(ax_loaded, B * 16 + 16))
                        v.wait_ge(xn_done, m * TT + TT)
                        for t in range(TT):
                            v.tensor_tensor(x_sb[:, par, t], x_sb[:, par, t], bias[:, :], ALU.add).then_inc(x_biased, 1)
                        v.wait_ge(kv_turned, B + 1)
                        kv = bank[1][:, 0:TT * 2 * HD].rearrange("p (t c d) -> p t c d", t=TT, c=2)
                        rotate(kv[:, :, 0], krot[:, 0], krot[:, 1], rot[:, :, 2], rot[:, :, 3], k_step, B * KSTEP, True)
                        ks = kstack[:, :, :].rearrange("p t (c e d) -> p t c e d", c=2, e=2)
                        kr = krot[:, 0].unsqueeze(2).to_broadcast([P, TT, 2, HD])
                        v.tensor_copy(ks[:, :, 0].bitcast(F32R), kr).then_inc(k_step, 1)
                        v.wait_ge(k_step, B * KSTEP + 5)
                        v.tensor_tensor(ks[:, :, 1], kr, ks[:, :, 0], ALU.subtract).then_inc(k_step, 1)
                        v.wait_ge(v_h_done, B + 1)
                        v.tensor_tensor(v_l[:, :, P - HD:P], kv[:, :, 1], v_h[:, :, P - HD:P].bitcast(F32),
                                        ALU.subtract).then_inc(v_done, 1)
                        v.wait_ge(stack_done, B * HEADS + HEADS)
                        for t in range(TT):
                            v.wait_ge(q_done, B * TT + t + 1)
                            cos = rot[:, t, 0].unsqueeze(1).to_broadcast([P, HEADS, HD])
                            sin = rot[:, t, 1].unsqueeze(1).to_broadcast([P, HEADS, HD])
                            rotate(heads_of(bank[4 + t][:, :]), heads_of(qrot[:, t]), heads_of(qtmp), cos, sin,
                                   q_step, (B * TT + t) * QSTEP, True)

                        def low_output(hg):
                            v.wait_ge(att_h_done, B * NHG + hg + 1)
                            v.tensor_tensor(att_l[:, hg], att, att_h[:, hg].bitcast(F32), ALU.subtract).then_inc(att_l_done, 1)

                        for u in range(HEADS + 2):
                            ended = u >= 3 and (u - 3) % HG == HG - 1
                            for i in range(TT):
                                if u < HEADS:
                                    e = u * TT + i
                                    v.wait_ge(score_done, B * NT + e + 1)
                                    v.tensor_reduce(nmax[:, u % 2, i:i + 1], bank[SCORES + e % 3][:, 0:width(i)], AX.X, ALU.max,
                                                    negate=True).then_inc(max_done, 1)
                                if i == 1 and ended:
                                    low_output((u - 3) // HG)
                                if 1 <= u <= HEADS:
                                    e = (u - 1) * TT + i
                                    v.wait_ge(pt_h_done, B * NT + e + 1)
                                    v.tensor_tensor(pt_l[:, (u - 1) % 2, 0:i + 1, i * P:(i + 1) * P],
                                                    bank[TURNS + e % 2][:, 0:width(i)].rearrange("p (j n) -> p j n", n=P),
                                                    pt_h[:, (u - 1) % 2, 0:i + 1, i * P:(i + 1) * P].bitcast(F32),
                                                    ALU.subtract).then_inc(pt_done, 1)
                            if u >= 1 and (u - 1) % HG == HG - 1 and u <= HEADS:
                                hg = (u - 1) // HG
                                v.wait_ge(exp_done, B * NT + u * TT)
                                v.reciprocal(rsum[:, :, :], sums[:, hg % 2]).then_inc(rsum_done, 1)
                                v.wait_ge(rsum_done, B * NHG + hg + 1)
                                v.tensor_copy(rwide[:, :, :, :], rsum[:, :, :].rearrange("p h t -> p t h").unsqueeze(3)
                                              .to_broadcast([P, TT, HG, HD])).then_inc(rwide_done, 1)
                            if u >= 2 and (u - 2) % HG == HG - 1:
                                hg = (u - 2) // HG
                                v.wait_ge(pv_done, B * HEADS + u - 1)
                                v.wait_ge(rt_done, B * NHG + hg + 1)
                                v.tensor_tensor(att, bank[OUTS + hg % 2][:, :], rt, ALU.mult).then_inc(att_done, 1)
                        low_output(NHG - 1)
                        v.wait_ge(x_biased, B * TT + TT)
                        for t in range(TT):
                            v.wait_ge(proj_done, B * TT + t + 1)
                            v.tensor_tensor(x_sb[:, par, t], x_sb[:, par, t], bank[t][:, :], ALU.add).then_inc(x_summed, 1)

        with nc.Block() as blk:
            @blk.gpsimd
            def _(g):
                g.memset(halves[:, :], -0.5).then_inc(const_pool, 1)
                for i, t in enumerate((ident, ident_b, mask_b)):
                    g.memset(t[:, :], 0.0).then_inc(const_pool, 1)
                g.wait_ge(const_pool, 4)
                for t in (ident, ident_b):
                    g.affine_select(out=t[:, :], in_=t[:, :], compare_op=ALU.not_equal, fill=1.0, base=0,
                                    pattern=[[-1, P]], channel_multiplier=1).then_inc(const_pool, 1)
                g.affine_select(out=mask_b[:, :], in_=mask_b[:, :], compare_op=ALU.is_ge, fill=MASKED, base=0,
                                pattern=[[-1, P]], channel_multiplier=1).then_inc(const_pool, 1)

        ffn_phase(0, x_in, x_mid[0], 0)
        attention_phase(x_mid[0], x_mid[1], GROUPS * NB)
        ffn_phase(1, x_mid[1], out, GROUPS * NB + BATCHES)


_INS = {}


def kernel(**inputs):
    import numpy as _np
    import concourse.bacc as _bacc
    from concourse import mybir as _mybir
    from concourse.bass_utils import run_bass_kernel_spmd as _run

    x = _np.ascontiguousarray(inputs["L0_attn_hidden_states"])
    B, S, D = x.shape
    I = inputs["L0_ffn_w_gate"].shape[1]
    NR, J = 4, 128
    NCH, K = I // (NR * J), D // 128

    def members(w):
        return _np.asarray(w).reshape(K, 128, NCH, J, NR).transpose(2, 4, 1, 0, 3)

    def by_k(w):
        w = _np.asarray(w).T
        return _np.ascontiguousarray(w.reshape(K, 128, -1).transpose(1, 0, 2))

    HD = inputs["L0_attn_w_kv"].shape[0] // 2
    f = _np.float32
    even = _np.arange(0, HD, 2, dtype=f)
    inv = f(1.0) / _np.power(f(10000.0), even / f(HD)).astype(f)
    t = _np.arange(S, dtype=f)
    ang = _np.concatenate([t[:, None] * inv[None, :]] * 2, axis=-1).astype(f)
    base = (even + f(0.4 * HD)) / f(1.4 * HD)
    sc = _np.power(base[None, :], ((t - S // 2) / f(128))[:, None]).astype(f)
    sc = _np.concatenate([sc, sc], axis=-1)
    sign = _np.concatenate([-_np.ones(HD // 2, f), _np.ones(HD // 2, f)])
    tables = _np.stack([_np.cos(ang) * sc / f(HD), _np.sin(ang) * sc * sign / f(HD),
                        _np.cos(ang) / sc, _np.sin(ang) * sign / sc], axis=1).astype(f)
    tables = _np.ascontiguousarray(tables.reshape(S // 128, 128, 4, HD).transpose(1, 0, 2, 3))

    arrays = {
        "x": x,
        "w_gu": _np.ascontiguousarray(_np.stack([members(inputs["L0_ffn_w_gate"]), members(inputs["L0_ffn_w_up"])], axis=3)),
        "w_d": _np.ascontiguousarray(_np.asarray(inputs["L0_ffn_w_down"]).reshape(NCH, J, NR, D).transpose(0, 2, 1, 3)),
        "w_q": by_k(inputs["L0_attn_w_q"]),
        "w_kv": by_k(inputs["L0_attn_w_kv"]),
        "w_p": by_k(inputs["L0_attn_w_proj"]),
        "b_p": _np.ascontiguousarray(_np.asarray(inputs["L0_attn_b_proj"]).reshape(1, D)),
        "rotary": tables,
    }
    nc = _bacc.Bacc("TRN2", target_bir_lowering=False, num_devices=1)
    args = [nc.dram_tensor(f"in_{n}", a.shape, _mybir.dt.from_np(a.dtype), kind="ExternalInput").ap()
            for n, a in arrays.items()]
    args.append(nc.dram_tensor("out_0", x.shape, _mybir.dt.from_np(x.dtype), kind="ExternalOutput").ap())
    macaron_kernel(nc, *args)
    r = _run(nc, [{f"in_{n}": a for n, a in arrays.items()}], core_ids=[0])
    return r.results[0]["out_0"]
```

```python
from contextlib import ExitStack

import concourse.bass as bass
from concourse import mybir

F32 = mybir.dt.float32
F32R = mybir.dt.float32r
BF16 = mybir.dt.bfloat16
ALU = mybir.AluOpType
ACT = mybir.ActivationFunctionType
AX = mybir.AxisListType

P = 128
EPS = 1e-5
MASKED = -3.0e38


def macaron_kernel(nc, x_in, w_gu, w_d, w_q, w_kv, w_p, b_p, rotary, out):
    BATCHES, S, D = x_in.shape
    KD = D // P
    NCH, NR = w_gu.shape[0], w_gu.shape[1]
    TT = S // P
    NB = 2
    GROUPS = BATCHES // NB
    STEPS = NCH * NB
    HD = w_kv.shape[2] // 2
    HEADS = D // HD
    HG = P // HD
    NHG = HEADS // HG
    assert TT == KD == NR == NHG == HG == 4

    x_mid = [nc.dram_tensor(f"x_mid{i}", [BATCHES, S, D], F32, kind="Internal").ap() for i in range(2)]

    def tiles(ap):
        return ap.rearrange("b (t p) d -> b p t d", p=P)

    at = [(nc.sbuf_base + 63) // 64 * 64]

    def place(name, shape, dt):
        size = 1
        for s in shape[1:]:
            size *= s
        size *= 2 if dt == BF16 else 4
        t = nc.alloc_sbuf_tensor_at(name, shape, dt, offset=at[0])
        at[0] += (size + 31) // 32 * 32
        return t

    ident = place("ident", [P, P], F32)
    ident_b = place("ident_b", [P, P], BF16)
    mask_b = place("mask_b", [P, P], BF16)
    halves = place("halves", [P, TT], F32)
    x_sb = place("x_sb", [P, 2, NB * TT, D], F32)
    xnt_h = place("xnt_h", [P, NB, KD, S], F32R)
    xnt_l = place("xnt_l", [P, NB, KD, S], F32R)
    xn = place("xn", [P, 2, D], F32)
    stats = place("stats", [P, TT, 6], F32)
    meanvar = place("meanvar", [P, TT, 2], F32)
    var_eps = place("var_eps", [P, TT], F32)
    rstd = place("rstd", [P, TT], F32)
    shared_end = at[0]

    wgu_h = place("wgu_h", [P, NR, 2, KD, P], F32R)
    wgu_l = place("wgu_l", [P, NR, 2, KD, P], F32R)
    wd_h = place("wd_h", [P, NR, D], F32R)
    wd_l = place("wd_l", [P, NR, D], F32R)
    raw_gu = place("raw_gu", [P, NR, 2, KD, P], F32)
    raw_d = place("raw_d", [P, NR, D], F32)
    sg = place("sg", [P, 2, S], F32)
    h = place("h", [P, NR, S], F32)
    mag = place("mag", [P, NR, S], F32)
    pmax = place("pmax", [P, 2, S], F32)
    first = place("first", [P, 2, S], BF16)
    kept_k = place("kept_k", [P, 2, S], BF16)
    kept_a = place("kept_a", [P, S], BF16)
    ksum = place("ksum", [P, 2, S], BF16)
    kdif = place("kdif", [P, 2, S], BF16)
    hs_h = place("hs_h", [P, NB, NR, S], F32R)
    hs_l = place("hs_l", [P, NB, NR, S], F32R)
    ffn_end = at[0]

    at[0] = shared_end
    wq_h = place("wq_h", [P, KD, D], F32R)
    wq_l = place("wq_l", [P, KD, D], F32R)
    wp_h = place("wp_h", [P, KD, D], F32R)
    wp_l = place("wp_l", [P, KD, D], F32R)
    wkv_h = place("wkv_h", [P, KD, 2 * HD], F32R)
    wkv_l = place("wkv_l", [P, KD, 2 * HD], F32R)
    rot = place("rot", [P, TT, 4, HD], F32)
    bias = place("bias", [P, D], F32)
    kvt = place("kvt", [2 * HD, S], F32)
    kvtok = place("kvtok", [P, TT, 2, HD], F32)
    krot = place("krot", [P, 2, TT, HD], F32)
    kstack = place("kstack", [P, TT, P], F32)
    kt = place("kt", [P, S], F32R)
    VW = 2 * (P - HD) + HD
    v_h = place("v_h", [P, TT, VW], F32R)
    v_l = place("v_l", [P, TT, VW], F32R)
    qrot = place("qrot", [P, TT, D], F32)
    qstack = place("qstack", [P, TT, HG, P], F32)
    qt = place("qt", [P, HG, S], F32R)
    nmax = place("nmax", [P, 2, TT], F32)
    sums = place("sums", [P, 2, HG, TT], F32)
    rsum = place("rsum", [P, HG, TT], F32)
    probs = place("probs", [P, 2, TT, S], F32)
    pt_h = place("pt_h", [P, 2, TT, S], F32R)
    pt_l = place("pt_l", [P, 2, TT, S], F32R)
    rwide = place("rwide", [P, TT, HG, HD], F32)
    att_end = at[0]
    assert max(ffn_end, att_end) <= nc.sbuf_usable_end, (ffn_end, att_end, nc.sbuf_usable_end)
    raw_q, raw_p = probs[:, 0], probs[:, 1]
    raw_kv = qrot[:, 0, 0:KD * 2 * HD].rearrange("p (k n) -> p k n", k=KD)
    att_h, att_l = xnt_h[:, 1], xnt_l[:, 1]
    rt, att, qtmp = x_sb[:, 0, TT], x_sb[:, 0, TT + 1], x_sb[:, 0, TT + 2]

    with ExitStack() as ctx:
        def sem(name):
            return ctx.enter_context(nc.semaphore(name))

        def sems(name, n):
            return [sem(f"{name}{i}") for i in range(n)]

        bank = [ctx.enter_context(nc.psum_tensor(f"bank{i}", [P, 512], F32)) for i in range(8)]

        const_pool = sem("const_pool")
        passed_vector, passed_gpsimd, passed_tensor = sem("passed_vector"), sem("passed_gpsimd"), sem("passed_tensor")
        x_loaded = sems("x_loaded", NB)
        x_stored = sem("x_stored")
        gu_loaded = sems("gu_loaded", NR)
        d_loaded = sems("d_loaded", NR)
        ln_stat = sem("ln_stat")
        rstd_step = sem("rstd_step")
        xn_done = sem("xn_done")
        xn_turned = sem("xn_turned")
        xnt_h_done = sem("xnt_h_done")
        xnt_done = sem("xnt_done")
        wgu_h_done = sem("wgu_h_done")
        wgu_done = sem("wgu_done")
        wd_h_done = sem("wd_h_done")
        wd_done = sem("wd_done")
        gate_done = sem("gate_done")
        up_done = sem("up_done")
        silu_done = sem("silu_done")
        h_done = sem("h_done")
        mag_done = sem("mag_done")
        rank_step = sem("rank_step")
        pruned = sem("pruned")
        hs_h_done = sem("hs_h_done")
        hs_done = sem("hs_done")
        down_done = sem("down_done")
        added = sem("added")
        RANK = 8
        aw_loaded = sems("aw_loaded", 5)
        aw_h_done = sem("aw_h_done")
        aw_done = sem("aw_done")
        pad_done = sem("pad_done")
        ax_loaded = sem("ax_loaded")
        kv_done = sem("kv_done")
        kvt_done = sem("kvt_done")
        kv_turned = sem("kv_turned")
        kvtok_done = sem("kvtok_done")
        k_step = sem("k_step")
        v_h_done = sem("v_h_done")
        v_done = sem("v_done")
        k_turned = sem("k_turned")
        kt_done = sem("kt_done")
        q_done = sem("q_done")
        q_step = sem("q_step")
        stack_h = sem("stack_h")
        stack_done = sem("stack_done")
        stack_turned = sem("stack_turned")
        qt_done = sem("qt_done")
        score_done = sem("score_done")
        max_done = sem("max_done")
        exp_done = sem("exp_done")
        p_turned = sem("p_turned")
        pt_h_done = sem("pt_h_done")
        pt_done = sem("pt_done")
        pv_done = sem("pv_done")
        rsum_done = sem("rsum_done")
        rwide_done = sem("rwide_done")
        r_turned = sem("r_turned")
        rt_done = sem("rt_done")
        att_done = sem("att_done")
        att_h_done = sem("att_h_done")
        att_l_done = sem("att_l_done")
        proj_done = sem("proj_done")
        x_biased = sem("x_biased")
        x_summed = sem("x_summed")
        ax_stored = sem("ax_stored")

        def passed(engine, mark):
            engine.sem_inc(mark, 1)

        def ln_vector(v, m, xt, slot, wait_x):
            wait_x(v)
            for t in range(TT):
                v.bn_stats(stats[:, t], xt(t)).then_inc(ln_stat, 1)
            v.wait_ge(ln_stat, m * 2 * TT + TT)
            passed(v, passed_vector)
            for t in range(TT):
                v.bn_aggr(meanvar[:, t], stats[:, t]).then_inc(ln_stat, 1)
            v.wait_ge(ln_stat, m * 2 * TT + 2 * TT)
            v.wait_ge(rstd_step, m * 2 + 2)
            for t in range(TT):
                v.wait_ge(xn_turned, m * TT + t + 1)
                v.tensor_scalar(xn[:, t % 2], xt(t), meanvar[:, t, 0:1], rstd[:, t:t + 1],
                                ALU.subtract, ALU.mult).then_inc(xn_done, 1)
                if t >= 1:
                    ln_low(v, m, t - 1, slot)
            ln_low(v, m, TT - 1, slot)

        def ln_low(v, m, t, slot):
            tok = slice(t * P, (t + 1) * P)
            v.wait_ge(xnt_h_done, m * TT + t + 1)
            v.tensor_tensor(xnt_l[:, slot, :, tok], bank[4 + t][:, :].rearrange("p (k n) -> p k n", k=KD),
                            xnt_h[:, slot, :, tok].bitcast(F32), ALU.subtract).then_inc(xnt_done, 1)

        def ln_scalar(a, m, slot):
            for t in range(TT):
                a.wait_ge(xn_turned, m * TT + t + 3)
                a.copy(xnt_h[:, slot, :, t * P:(t + 1) * P],
                       bank[4 + t][:, :].rearrange("p (k n) -> p k n", k=KD)).then_inc(xnt_h_done, 1)

        def ln_tensor(pe, m, bank_free):
            for t in range(TT):
                bank_free(t)
                pe.wait_ge(xn_done, m * TT + t + 1)
                for k in range(KD):
                    last = pe.transpose(bank[4 + t][:, k * P:(k + 1) * P], xn[:, t % 2, k * P:(k + 1) * P],
                                        ident[:, :])
                last.then_inc(xn_turned, 1)

        def ln_gpsimd(g, m):
            g.wait_ge(ln_stat, m * 2 * TT + 2 * TT)
            passed(g, passed_gpsimd)
            g.tensor_scalar(var_eps[:, :], meanvar[:, :, 1], EPS, None, ALU.add).then_inc(rstd_step, 1)
            g.wait_ge(rstd_step, m * 2 + 1)
            g.tensor_tensor(rstd[:, :], var_eps[:, :], halves[:, :], ALU.pow).then_inc(rstd_step, 1)

        def ffn_phase(phase, src, dst, m0):
            n0 = phase * GROUPS * STEPS
            c0 = phase * GROUPS * NCH
            src_t, dst_t = tiles(src), tiles(dst)
            block = nc.Block()

            def body(block):
                @block.sync
                def _(sp):
                    def load_gu(load, c):
                        for r in range(NR):
                            if isinstance(load, int):
                                if load > 0:
                                    sp.wait_ge(wgu_done, load * NR)
                            else:
                                sp.wait_ge(wgu_done, (load - 1) * NR + r + 1)
                            sp.dma_start(raw_gu[:, r], w_gu[c, r]).then_inc(gu_loaded[r], 16)

                    def load_d(c):
                        for r in range(NR):
                            sp.dma_start(raw_d[:, r], w_d[c, r]).then_inc(d_loaded[r], 16)

                    def load_x(g, par):
                        for b in range(NB):
                            sp.dma_start(x_sb[:, par, b * TT:(b + 1) * TT], src_t[g * NB + b]).then_inc(x_loaded[b], 16)

                    def store_x(g):
                        for b in range(NB):
                            sp.wait_ge(added, (n0 + g * STEPS + STEPS - NB + b) * TT + 2 * TT)
                            sp.dma_start(dst_t[g * NB + b], x_sb[:, g % 2, b * TT:(b + 1) * TT]).then_inc(x_stored, 16)

                    def group_weights(g):
                        with sp.Fori(0, NCH) as c:
                            chunk = g * NCH + c
                            load_gu(chunk + (c0 + phase + 1), (c + 1) % NCH)
                            for r in range(NR):
                                sp.wait_ge(wd_done, (chunk + c0) * NR + r + 1)
                                sp.dma_start(raw_d[:, r], w_d[(c + 1) % NCH, r]).then_inc(d_loaded[r], 16)

                    load_x(0, 0)
                    load_gu(c0 + phase, 0)
                    load_d(0)
                    for b in range(NB):
                        sp.wait_ge(x_loaded[b], (phase * GROUPS + 1) * 16)
                    load_x(1, 1)
                    group_weights(0)
                    store_x(0)
                    with sp.Fori(1, GROUPS - 1) as g:
                        sp.wait_ge(x_stored, (g + phase * GROUPS) * NB * 16)
                        load_x(g + 1, (g + 1) % 2)
                        group_weights(g)
                        store_x(g)
                    group_weights(GROUPS - 1)
                    store_x(GROUPS - 1)
                    sp.wait_ge(x_stored, (phase + 1) * GROUPS * NB * 16)
                    for r in range(NR):
                        sp.wait_ge(d_loaded[r], (c0 + phase + GROUPS * NCH + 1) * 16)

                @block.gpsimd
                def _(g):
                    with g.Fori(0, GROUPS * NB) as m:
                        ln_gpsimd(g, m + m0)

                @block.tensor
                def _(pe):
                    def gate_up(n, b, cw):
                        for r in range(NR):
                            if b == 0:
                                pe.wait_ge(wgu_done, cw * NR + r + 1)
                            for kind, done, free, banks in ((0, gate_done, silu_done, 0), (1, up_done, h_done, 2)):
                                pe.wait_ge(free, n * NR + r + 1)
                                ps = bank[banks + r % 2][:, :]
                                i = 0
                                for k in range(KD):
                                    for w, xs in ((wgu_h, xnt_h), (wgu_h, xnt_l), (wgu_l, xnt_h)):
                                        last = pe.matmul(ps, w[:, r, kind, k], xs[:, b, k], start=(i == 0),
                                                         stop=(i == 3 * KD - 1))
                                        i += 1
                                last.then_inc(done, 1)

                    def down(n, b, chunk):
                        pe.wait_ge(hs_done, n * NR + 2 * NR)
                        if b == 0:
                            pe.wait_ge(wd_done, chunk * NR + NR)
                        for t in range(TT):
                            pe.wait_ge(added, n * TT + t + 1)
                            tok = slice(t * P, (t + 1) * P)
                            i = 0
                            for r in range(NR):
                                for hs, w in ((hs_h, wd_h), (hs_h, wd_l), (hs_l, wd_h)):
                                    last = pe.matmul(bank[4 + t][:, :], hs[:, b, r, tok], w[:, r], start=(i == 0),
                                                     stop=(i == 3 * NR - 1))
                                    i += 1
                            last.then_inc(down_done, 1)

                    if phase == 0:
                        pe.sem_inc(xn_turned, 2)
                        pe.sem_inc(down_done, TT)
                        pe.wait_ge(const_pool, 7)
                    with pe.Fori(0, GROUPS) as g:
                        n = g * STEPS + n0
                        m = g * NB + m0
                        ln_tensor(pe, m, lambda t: pe.wait_ge(added, n * TT + t + 1))
                        ln_tensor(pe, m + 1, lambda t: pe.wait_ge(xnt_done, m * TT + t + 1))
                        pe.wait_ge(xnt_done, m * TT + 2 * TT)
                        cw = g * NCH + (c0 + phase)
                        chunk = g * NCH + c0
                        gate_up(n, 0, cw)
                        gate_up(n + 1, 1, cw)
                        down(n, 0, chunk)
                        with pe.Fori(1, NCH) as c:
                            nn = n + c * NB
                            gate_up(nn, 0, cw + c)
                            down(nn - 1, 1, chunk + c - 1)
                            gate_up(nn + 1, 1, cw + c)
                            down(nn, 0, chunk + c)
                        down(n + STEPS - 1, 1, chunk + NCH - 1)

                @block.scalar
                def _(a):
                    def cut_gu(load, r):
                        a.wait_ge(gu_loaded[r], load * 16 + 16)
                        a.copy(wgu_h[:, r], raw_gu[:, r]).then_inc(wgu_h_done, 1)

                    def step(n, b, chunk, load):
                        for r in range(NR):
                            a.wait_ge(gate_done, n * NR + r + 1)
                            a.wait_ge(h_done, n * NR + r + 1)
                            a.activation(sg[:, r % 2], bank[r % 2][:, :], ACT.Silu).then_inc(silu_done, 1)
                            if b == 1:
                                if r == 0:
                                    a.wait_ge(down_done, n * TT)
                                a.wait_ge(d_loaded[r], (chunk + phase) * 16 + 16)
                                a.copy(wd_h[:, r], raw_d[:, r]).then_inc(wd_h_done, 1)
                                if r >= 1:
                                    cut_gu(load, r - 1)
                            a.wait_ge(h_done, n * NR + r + 3)
                            a.activation(mag[:, r], h[:, r], ACT.Abs).then_inc(mag_done, 1)
                        if b == 1:
                            a.wait_ge(up_done, n * NR + NR)
                            cut_gu(load, NR - 1)
                        for r in range(NR):
                            a.wait_ge(pruned, n * NR + r + 1)
                            a.copy(hs_h[:, b, r], h[:, r]).then_inc(hs_h_done, 1)

                    if phase == 0:
                        a.sem_inc(silu_done, 2)
                    for r in range(NR):
                        cut_gu(c0 + phase, r)
                    with a.Fori(0, GROUPS) as g:
                        ln_scalar(a, g * NB + m0, 0)
                        ln_scalar(a, g * NB + (m0 + 1), 1)
                        with a.Fori(0, NCH) as c:
                            n = g * STEPS + c * NB + n0
                            chunk = g * NCH + c + c0
                            step(n, 0, chunk, None)
                            step(n + 1, 1, chunk, chunk + (phase + 1))

                @block.vector
                def _(v):
                    def cut_gu(load, r):
                        v.wait_ge(wgu_h_done, load * NR + r + 1)
                        v.tensor_tensor(wgu_l[:, r], raw_gu[:, r], wgu_h[:, r].bitcast(F32),
                                        ALU.subtract).then_inc(wgu_done, 1)

                    def add_down(n, b, par):
                        for t in range(TT):
                            v.wait_ge(down_done, n * TT + t + 1 + TT)
                            x = x_sb[:, par, b * TT + t]
                            v.scalar_tensor_tensor(out=x, in0=bank[4 + t][:, :], scalar=0.5, in1=x, op0=ALU.mult,
                                                   op1=ALU.add).then_inc(added, 1)

                    def step(n, b, chunk, load, before, par):
                        v.wait_ge(hs_done, n * NR + NR)
                        for r in range(NR):
                            v.wait_ge(up_done, n * NR + r + 1)
                            v.wait_ge(silu_done, n * NR + r + 3)
                            v.tensor_tensor(h[:, r], bank[2 + r % 2][:, :], sg[:, r % 2], ALU.mult).then_inc(h_done, 1)
                            if b == 1:
                                v.wait_ge(wd_h_done, chunk * NR + r + 1)
                                v.tensor_tensor(wd_l[:, r], raw_d[:, r], wd_h[:, r].bitcast(F32),
                                                ALU.subtract).then_inc(wd_done, 1)
                                if r >= 1:
                                    cut_gu(load, r - 1)
                        if b == 1:
                            cut_gu(load, NR - 1)
                        pair = mag[:, :, :].rearrange("p (a e) s -> p a e s", e=2)
                        base = n * RANK
                        v.wait_ge(mag_done, n * NR + NR)
                        v.tensor_tensor(first[:, :, :], pair[:, :, 0], pair[:, :, 1], ALU.is_ge).then_inc(rank_step, 1)
                        v.tensor_tensor(pmax[:, :, :], pair[:, :, 0], pair[:, :, 1], ALU.max).then_inc(rank_step, 1)
                        v.tensor_tensor(pair[:, :, 0], pair[:, :, 0], pair[:, :, 1], ALU.min).then_inc(rank_step, 1)
                        v.wait_ge(rank_step, base + 3)
                        v.tensor_tensor(kept_k[:, 0], mag[:, 0], pmax[:, 1], ALU.is_ge).then_inc(rank_step, 1)
                        v.tensor_tensor(kept_k[:, 1], pmax[:, 0], mag[:, 2], ALU.is_ge).then_inc(rank_step, 1)
                        v.wait_ge(rank_step, base + 5)
                        v.tensor_tensor(kept_a[:, :], kept_k[:, 0], kept_k[:, 1], ALU.add).then_inc(rank_step, 1)
                        v.wait_ge(rank_step, base + 6)
                        wide = kept_a[:, :].unsqueeze(1).to_broadcast([P, 2, S])
                        v.tensor_tensor(ksum[:, :, :], wide, first[:, :, :], ALU.add).then_inc(rank_step, 1)
                        v.tensor_tensor(kdif[:, :, :], wide, first[:, :, :], ALU.subtract).then_inc(rank_step, 1)
                        v.wait_ge(rank_step, base + 8)
                        rules = ((ksum[:, 0], 2.0, ALU.is_ge), (kdif[:, 0], 1.0, ALU.is_ge),
                                 (kdif[:, 1], 0.0, ALU.is_le), (ksum[:, 1], 1.0, ALU.is_le))
                        for r, (count, least, op) in enumerate(rules):
                            v.scalar_tensor_tensor(out=h[:, r], in0=count, scalar=least, in1=h[:, r], op0=op,
                                                   op1=ALU.mult).then_inc(pruned, 1)
                        if before:
                            add_down(n - 1, 1 - b, par)
                        for r in range(NR):
                            v.wait_ge(hs_h_done, n * NR + r + 1)
                            v.tensor_tensor(hs_l[:, b, r], h[:, r], hs_h[:, b, r].bitcast(F32),
                                            ALU.subtract).then_inc(hs_done, 1)

                    if phase == 0:
                        v.sem_inc(h_done, 2)
                        v.sem_inc(hs_done, NR)
                        v.sem_inc(added, TT)
                    for r in range(NR):
                        cut_gu(c0 + phase, r)
                    with v.Fori(0, GROUPS) as g:
                        par = g % 2
                        for b in range(NB):
                            ln_vector(v, g * NB + (m0 + b), lambda t: x_sb[:, par, b * TT + t], b,
                                      lambda v: v.wait_ge(x_loaded[b], (g + phase * GROUPS) * 16 + 16))
                        n = g * STEPS + n0
                        chunk = g * NCH + c0
                        step(n, 0, chunk, None, False, par)
                        step(n + 1, 1, chunk, chunk + (phase + 1), True, par)
                        with v.Fori(1, NCH) as c:
                            step(n + c * NB, 0, chunk + c, None, True, par)
                            step(n + c * NB + 1, 1, chunk + c, chunk + c + (phase + 1), True, par)
                        add_down(n + STEPS - 1, 1, par)

            with block as blk:
                body(blk)

        def attention_phase(src, dst, m0):
            src_t, dst_t = tiles(src), tiles(dst)
            NT = HEADS * TT
            SCORES, TURNS, OUTS, SPARE = 0, 3, 5, 7
            KSTEP, QSTEP = 6, 4
            HALF = HD // 2
            meets = [(j * P if j < TT - 1 else (TT - 2) * P) for j in range(TT)]
            STATS = [7 * TT + t for t in range(TT)]
            NORMS = [(9 + t) * TT for t in range(TT)]
            TURNX = [(9 + t) * TT + 1 for t in range(TT)]
            PROJ_KV, TURN_KV = 13 * TT + 1, 14 * TT + 1
            PROJ_Q = [15 * TT, 15 * TT + 2, 16 * TT + 2]
            TURN_K = 16 * TT

            def width(i):
                return (i + 1) * P

            def heads_of(ap):
                return ap.rearrange("p (h d) -> p h d", d=HD)

            spare = bank[SPARE]

            with nc.Block() as blk:
                @blk.sync
                def _(sp):
                    sp.dma_start(x_sb[:, 0, 0:TT], src_t[0]).then_inc(ax_loaded, 16)
                    sp.dma_start(raw_kv, w_kv).then_inc(aw_loaded[0], 16)
                    sp.dma_start(raw_q, w_q).then_inc(aw_loaded[1], 16)
                    sp.dma_start(rot[:, :, :, :], rotary).then_inc(aw_loaded[2], 16)
                    sp.dma_start(raw_p, w_p).then_inc(aw_loaded[3], 16)
                    sp.dma_start(bias[:, :], b_p.to_broadcast([P, D])).then_inc(aw_loaded[4], 16)
                    sp.wait_ge(ax_loaded, 16)
                    sp.dma_start(x_sb[:, 1, 0:TT], src_t[1]).then_inc(ax_loaded, 16)

                    def store(B, par):
                        for t in range(TT):
                            sp.wait_ge(x_summed, B * TT + t + 1 + TT)
                            sp.dma_start(dst_t[B, :, t], x_sb[:, par, t]).then_inc(ax_stored, 16)

                    with sp.Fori(0, BATCHES - 2) as B:
                        store(B, B % 2)
                        sp.wait_ge(ax_stored, (B * TT + TT) * 16)
                        sp.wait_ge(ax_loaded, (B + 2) * 16)
                        sp.dma_start(x_sb[:, B % 2, 0:TT], src_t[B + 2]).then_inc(ax_loaded, 16)
                    for B in range(BATCHES - 2, BATCHES):
                        store(B, B % 2)
                    sp.wait_ge(ax_stored, BATCHES * TT * 16)

                @blk.gpsimd
                def _(g):
                    def stack_head(B, w):
                        if w == 0:
                            g.wait_ge(q_step, (B + 1) * QSTEP * TT)
                            passed(g, passed_gpsimd)
                        g.wait_ge(stack_turned, B * HEADS + w + 1)
                        passed(g, passed_gpsimd)
                        slot = qstack[:, :, w % HG].rearrange("p t (e c d) -> p t e c d", e=2, c=2)
                        q = qrot[:, :, w * HD:(w + 1) * HD].unsqueeze(2).to_broadcast([P, TT, 2, HD])
                        g.tensor_copy(slot[:, :, :, 0].bitcast(F32R), q).then_inc(stack_h, 1)
                        g.wait_ge(stack_h, B * HEADS + w + 1)
                        g.tensor_tensor(slot[:, :, :, 1], q, slot[:, :, :, 0], ALU.subtract).then_inc(stack_done, 1)

                    def batch(B, front):
                        for w in range(2, HEADS):
                            stack_head(B, w)
                            if front and w == HEADS - 3:
                                ln_gpsimd(g, B + (m0 + 1))
                        if front:
                            stack_head(B + 1, 0)
                            stack_head(B + 1, 1)

                    g.sem_inc(stack_done, HEADS)
                    ln_gpsimd(g, m0)
                    for t in (v_h, v_l):
                        g.memset(t[:, :, :].bitcast(F32), 0.0).then_inc(pad_done, 1)
                    for t in (pt_h, pt_l):
                        g.memset(t[:, :, TT - 1, meets[-1]:(TT - 1) * P].bitcast(F32), 0.0).then_inc(pad_done, 1)
                    stack_head(0, 0)
                    stack_head(0, 1)
                    with g.Fori(0, BATCHES - 1) as B:
                        batch(B, True)
                    batch(BATCHES - 1, False)

                @blk.tensor
                def _(pe):
                    class Spare:
                        sem, value = None, None

                    def take_spare(drained_by, value):
                        if Spare.sem is not None:
                            pe.wait_ge(Spare.sem, Spare.value)
                        Spare.sem, Spare.value = drained_by, value

                    def project_x(ps, w_hi, w_lo, t=None):
                        i = 0
                        for k in range(KD):
                            for a, b in ((w_hi, xnt_h), (w_lo, xnt_h), (w_hi, xnt_l)):
                                x = b[:, 0, k] if t is None else b[:, 0, k, t * P:(t + 1) * P]
                                still, moving = (a[:, k], x) if t is None else (x, a[:, k])
                                last = pe.matmul(ps, still, moving, start=(i == 0), stop=(i == 3 * KD - 1))
                                i += 1
                        return last

                    def turn_x(B, t):
                        pe.wait_ge(xn_done, (B + m0) * TT + t + 1)
                        take_spare(xnt_done, (B + m0) * TT + t + 1)
                        for k in range(KD):
                            last = pe.transpose(spare[:, k * P:(k + 1) * P], xn[:, t % 2, k * P:(k + 1) * P], ident[:, :])
                        last.then_inc(xn_turned, 1)

                    def project_kv(B):
                        take_spare(kvt_done, B + 1)
                        project_x(spare[0:2 * HD, :], wkv_h, wkv_l).then_inc(kv_done, 1)

                    def turn_kv(B):
                        take_spare(kvtok_done, B + 1)
                        passed(pe, passed_tensor)
                        for t in range(TT):
                            last = pe.transpose(spare[:, t * 2 * HD:(t + 1) * 2 * HD], kvt[:, t * P:(t + 1) * P],
                                                ident[0:2 * HD, 0:2 * HD])
                        last.then_inc(kv_turned, 1)

                    def turn_k(B):
                        pe.wait_ge(k_step, B * KSTEP + KSTEP)
                        take_spare(kt_done, B + 1)
                        for t in range(TT):
                            last = pe.transpose(spare[:, t * P:(t + 1) * P], kstack[:, t], ident[:, :])
                        last.then_inc(k_turned, 1)

                    def project_q(B, t):
                        take_spare(q_step, (B * TT + t) * QSTEP + QSTEP - 1)
                        project_x(spare[:, :], wq_h, wq_l, t).then_inc(q_done, 1)

                    def turn_stack(B, w):
                        pe.wait_ge(stack_done, B * HEADS + w + 1 + HEADS)
                        take_spare(qt_done, B * HEADS + w + 1)
                        for t in range(TT):
                            last = pe.transpose(spare[:, t * P:(t + 1) * P], qstack[:, t, w % HG], ident[:, :])
                        last.then_inc(stack_turned, 1)

                    def turn_sums(B, hg):
                        pe.wait_ge(rwide_done, B * NHG + hg + 1)
                        take_spare(rt_done, B * NHG + hg + 1)
                        for t in range(TT):
                            last = pe.transpose(spare[:, t * P:(t + 1) * P],
                                                rwide[:, t].rearrange("p h d -> p (h d)"), ident[:, :])
                        last.then_inc(r_turned, 1)

                    def scores(B, e):
                        u, i = e // TT, e % TT
                        if e >= 3:
                            pe.wait_ge(exp_done, B * NT + e - 2)
                        else:
                            pe.wait_ge(x_summed, B * TT + e + 1)
                        if e == 0:
                            pe.wait_ge(kt_done, B + 1)
                        if i == 0:
                            pe.wait_ge(qt_done, B * HEADS + u + 1)
                        ps = bank[SCORES + e % 3]
                        n = max(width(i), 2 * P)
                        pe.matmul(ps[:, 0:n], qt[:, u % HG, i * P:(i + 1) * P], kt[:, 0:n], start=True, stop=False)
                        pe.matmul(ps[:, i * P:width(i)], ident_b[:, :], mask_b[:, :], start=False,
                                  stop=True).then_inc(score_done, 1)

                    def turn_probs(B, e):
                        u, i = e // TT, e % TT
                        pe.wait_ge(exp_done, B * NT + e + 1)
                        if e >= 2:
                            pe.wait_ge(pt_done, B * NT + e - 1)
                        else:
                            pe.wait_ge(x_summed, B * TT + TT)
                        for j in range(i + 1):
                            last = pe.transpose(bank[TURNS + e % 2][:, j * P:(j + 1) * P],
                                                probs[:, u % 2, i, j * P:(j + 1) * P], ident[:, :])
                        last.then_inc(p_turned, 1)

                    def weigh(B, e):
                        u, j = e // TT, e % TT
                        hg, s = u // HG, u % HG
                        if e == 0:
                            pe.wait_ge(v_done, B + 1)
                        if j == 0:
                            pe.wait_ge(pt_done, B * NT + u * TT + TT)
                            if s == 0 and hg >= 2:
                                pe.wait_ge(att_done, B * NHG + hg - 1)
                        window = slice((HG - 1 - s) * HD, (HG - 1 - s) * HD + P)
                        a = meets[j]
                        for i, (v, pt) in enumerate(((v_h, pt_h), (v_l, pt_h), (v_h, pt_l))):
                            last = pe.matmul(bank[OUTS + hg % 2][:, a:S], v[:, j, window], pt[:, u % 2, j, a:S],
                                             start=(s == 0 and j == 0 and i == 0),
                                             stop=(s == HG - 1 and j == TT - 1 and i == 2))
                        if j == TT - 1:
                            last.then_inc(pv_done, 1)

                    def project_out(t):
                        i = 0
                        for k in range(KD):
                            for a, w in ((att_h, wp_h), (att_h, wp_l), (att_l, wp_h)):
                                last = pe.matmul(bank[t][:, :], a[:, k, t * P:(t + 1) * P], w[:, k],
                                                 start=(i == 0), stop=(i == 3 * KD - 1))
                                i += 1
                        last.then_inc(proj_done, 1)

                    def batch(B, front):
                        nxt = B + 1
                        Spare.sem, Spare.value = qt_done, B * HEADS + 2
                        scores(B, 0)
                        for e in range(NT + 2 * TT):
                            u, i = e // TT, e % TT
                            if e + 1 < NT:
                                scores(B, e + 1)
                            if TT <= e < NT + TT:
                                turn_probs(B, e - TT)
                            if front:
                                if e in TURNX:
                                    turn_x(nxt, TURNX.index(e))
                                if e == PROJ_KV:
                                    pe.wait_ge(xnt_done, (nxt + m0) * TT + TT)
                                    project_kv(nxt)
                                if e == TURN_KV:
                                    turn_kv(nxt)
                                if e == TURN_K:
                                    turn_k(nxt)
                                if e in PROJ_Q:
                                    project_q(nxt, PROJ_Q.index(e))
                            if e >= 2 * TT:
                                weigh(B, e - 2 * TT)
                            if i == TT - 1:
                                if u + 2 < HEADS:
                                    turn_stack(B, u + 2)
                                if u >= 1 and (u - 1) % HG == HG - 1:
                                    turn_sums(B, (u - 1) // HG)
                        if front:
                            project_q(nxt, TT - 1)
                        pe.wait_ge(att_l_done, B * NHG + NHG)
                        for t in range(TT):
                            project_out(t)
                            if front and t >= TT - 2:
                                turn_stack(nxt, t - (TT - 2))

                    pe.sem_inc(stack_turned, HG)
                    for t in range(TT):
                        turn_x(0, t)
                    pe.wait_ge(xnt_done, m0 * TT + TT)
                    pe.wait_ge(aw_done, 2)
                    project_kv(0)
                    project_q(0, 0)
                    turn_kv(0)
                    project_q(0, 1)
                    project_q(0, 2)
                    turn_k(0)
                    project_q(0, 3)
                    turn_stack(0, 0)
                    turn_stack(0, 1)
                    pe.wait_ge(aw_done, 3)
                    with pe.Fori(0, BATCHES - 1) as B:
                        batch(B, True)
                    batch(BATCHES - 1, False)

                @blk.scalar
                def _(a):
                    def hi_x(B, t):
                        a.wait_ge(xn_turned, (B + m0) * TT + t + 3)
                        a.copy(xnt_h[:, 0, :, t * P:(t + 1) * P],
                               spare[:, :].rearrange("p (k n) -> p k n", k=KD)).then_inc(xnt_h_done, 1)

                    def drain_kv(B):
                        a.wait_ge(kv_done, B + 1)
                        a.copy(kvt[:, :], spare[0:2 * HD, :]).then_inc(kvt_done, 1)

                    def drain_kvtok(B):
                        a.wait_ge(kv_turned, B + 1)
                        a.copy(kvtok[:, :, :, :], spare[:, 0:TT * 2 * HD].rearrange("p (t c d) -> p t c d", t=TT, c=2)
                               ).then_inc(kvtok_done, 1)

                    def drain_k(B):
                        a.wait_ge(k_turned, B + 1)
                        a.copy(kt[:, :], spare[:, :]).then_inc(kt_done, 1)

                    def hi_v(B):
                        a.wait_ge(kvtok_done, B + 1)
                        a.copy(v_h[:, :, P - HD:P], kvtok[:, :, 1]).then_inc(v_h_done, 1)

                    def queries(B, w):
                        a.wait_ge(stack_turned, B * HEADS + w + 1 + HG)
                        a.copy(qt[:, w % HG], spare[:, :]).then_inc(qt_done, 1)

                    def cast_output(B, hg):
                        a.wait_ge(att_done, B * NHG + hg + 1)
                        a.copy(att_h[:, hg], att).then_inc(att_h_done, 1)

                    def batch(B, front):
                        nxt = B + 1
                        for e in range(NT + 2 * TT):
                            u, i = e // TT, e % TT
                            if TT <= e < NT + TT:
                                f = e - TT
                                a.wait_ge(p_turned, B * NT + f + 1)
                                a.copy(pt_h[:, (f // TT) % 2, 0:i + 1, i * P:(i + 1) * P],
                                       bank[TURNS + f % 2][:, 0:width(i)].rearrange("p (j n) -> p j n", n=P)
                                       ).then_inc(pt_h_done, 1)
                            if e < NT:
                                a.wait_ge(max_done, B * NT + e + 1)
                                a.activation(probs[:, u % 2, i, 0:width(i)], bank[SCORES + e % 3][:, 0:width(i)], ACT.Exp,
                                             bias=nmax[:, u % 2, i:i + 1],
                                             accum_out=sums[:, (u // HG) % 2, u % HG, i:i + 1]).then_inc(exp_done, 1)
                            if i == 0 and u >= 3 and (u - 3) % HG == HG - 1:
                                cast_output(B, (u - 3) // HG)
                            if front:
                                if e in TURNX:
                                    hi_x(nxt, TURNX.index(e))
                                if e == PROJ_KV:
                                    drain_kv(nxt)
                                if e == TURN_KV:
                                    drain_kvtok(nxt)
                                if e == TURN_K:
                                    drain_k(nxt)
                            if i == TT - 1:
                                if u + 2 < HEADS:
                                    queries(B, u + 2)
                                if u >= 1 and (u - 1) % HG == HG - 1:
                                    a.wait_ge(r_turned, B * NHG + (u - 1) // HG + 1)
                                    a.copy(rt, spare[:, :]).then_inc(rt_done, 1)
                        cast_output(B, NHG - 1)
                        if front:
                            a.wait_ge(pv_done, B * HEADS + HEADS)
                            hi_v(nxt)
                            queries(nxt, 0)
                            queries(nxt, 1)

                    for i, (ld, hi, raw) in enumerate(((0, wkv_h, raw_kv), (1, wq_h, raw_q))):
                        a.wait_ge(aw_loaded[ld], 16)
                        a.copy(hi[:, :, :], raw).then_inc(aw_h_done, 1)
                    for t in range(TT):
                        hi_x(0, t)
                    drain_kv(0)
                    drain_kvtok(0)
                    a.wait_ge(pad_done, 4)
                    hi_v(0)
                    drain_k(0)
                    a.wait_ge(aw_loaded[3], 16)
                    a.copy(wp_h[:, :, :], raw_p).then_inc(aw_h_done, 1)
                    queries(0, 0)
                    queries(0, 1)
                    with a.Fori(0, BATCHES - 1) as B:
                        batch(B, True)
                    batch(BATCHES - 1, False)

                @blk.vector
                def _(v):
                    def cut_weights(i, hi, lo, raw):
                        v.wait_ge(aw_h_done, i + 1)
                        v.tensor_tensor(lo[:, :, :], raw, hi[:, :, :].bitcast(F32), ALU.subtract).then_inc(aw_done, 1)

                    def rotate(x, dst, tmp, cos, sin, step, base):
                        v.tensor_tensor(dst, x, cos, ALU.mult).then_inc(step, 1)
                        v.tensor_tensor(tmp[:, :, 0:HALF], x[:, :, HALF:HD], sin[:, :, 0:HALF], ALU.mult).then_inc(step, 1)
                        v.tensor_tensor(tmp[:, :, HALF:HD], x[:, :, 0:HALF], sin[:, :, HALF:HD], ALU.mult).then_inc(step, 1)
                        v.wait_ge(step, base + 3)
                        v.tensor_tensor(dst, dst, tmp, ALU.add).then_inc(step, 1)
                        v.wait_ge(step, base + 4)

                    def x_of(B, t):
                        return x_sb[:, B % 2, t]

                    def stat(B, t):
                        if t == 0:
                            v.wait_ge(ax_loaded, B * 16 + 16)
                        v.bn_stats(stats[:, t], x_of(B, t)).then_inc(ln_stat, 1)

                    def aggregate(B):
                        v.wait_ge(ln_stat, (B + m0) * 2 * TT + TT)
                        passed(v, passed_vector)
                        for t in range(TT):
                            v.bn_aggr(meanvar[:, t], stats[:, t]).then_inc(ln_stat, 1)

                    def normalise(B, t):
                        m = B + m0
                        if t == 0:
                            v.wait_ge(ln_stat, m * 2 * TT + 2 * TT)
                            v.wait_ge(rstd_step, m * 2 + 2)
                        v.wait_ge(xn_turned, m * TT + t + 1)
                        v.tensor_scalar(xn[:, t % 2], x_of(B, t), meanvar[:, t, 0:1], rstd[:, t:t + 1],
                                        ALU.subtract, ALU.mult).then_inc(xn_done, 1)

                    def lo_x(B, t):
                        m = B + m0
                        tok = slice(t * P, (t + 1) * P)
                        v.wait_ge(xnt_h_done, m * TT + t + 1)
                        v.tensor_tensor(xnt_l[:, 0, :, tok], spare[:, :].rearrange("p (k n) -> p k n", k=KD),
                                        xnt_h[:, 0, :, tok].bitcast(F32), ALU.subtract).then_inc(xnt_done, 1)

                    def add_bias(B, t):
                        v.wait_ge(xn_done, (B + m0) * TT + t + 1)
                        v.tensor_tensor(x_of(B, t), x_of(B, t), bias[:, :], ALU.add).then_inc(x_biased, 1)

                    def keys(B):
                        v.wait_ge(kvtok_done, B + 1)
                        rotate(kvtok[:, :, 0], krot[:, 0], krot[:, 1], rot[:, :, 2], rot[:, :, 3], k_step, B * KSTEP)
                        ks = kstack[:, :, :].rearrange("p t (c e d) -> p t c e d", c=2, e=2)
                        kr = krot[:, 0].unsqueeze(2).to_broadcast([P, TT, 2, HD])
                        v.tensor_copy(ks[:, :, 0].bitcast(F32R), kr).then_inc(k_step, 1)
                        v.wait_ge(k_step, B * KSTEP + 5)
                        v.tensor_tensor(ks[:, :, 1], kr, ks[:, :, 0], ALU.subtract).then_inc(k_step, 1)

                    def lo_v(B):
                        v.wait_ge(v_h_done, B + 1)
                        v.tensor_tensor(v_l[:, :, P - HD:P], kvtok[:, :, 1], v_h[:, :, P - HD:P].bitcast(F32),
                                        ALU.subtract).then_inc(v_done, 1)

                    def rotate_q(B, t):
                        if t == 0:
                            v.wait_ge(stack_done, B * HEADS + HEADS)
                        v.wait_ge(q_done, B * TT + t + 1)
                        cos = rot[:, t, 0].unsqueeze(1).to_broadcast([P, HEADS, HD])
                        sin = rot[:, t, 1].unsqueeze(1).to_broadcast([P, HEADS, HD])
                        rotate(heads_of(spare[:, :]), heads_of(qrot[:, t]), heads_of(qtmp), cos, sin,
                               q_step, (B * TT + t) * QSTEP)

                    def low_output(B, hg):
                        v.wait_ge(att_h_done, B * NHG + hg + 1)
                        v.tensor_tensor(att_l[:, hg], att, att_h[:, hg].bitcast(F32), ALU.subtract).then_inc(att_l_done, 1)

                    def row_max(B, e):
                        u, i = e // TT, e % TT
                        v.wait_ge(score_done, B * NT + e + 1)
                        v.tensor_reduce(nmax[:, u % 2, i:i + 1], bank[SCORES + e % 3][:, 0:width(i)], AX.X, ALU.max,
                                        negate=True).then_inc(max_done, 1)

                    def batch(B, front):
                        nxt = B + 1
                        row_max(B, 0)
                        for e in range(NT + 2 * TT):
                            u, i = e // TT, e % TT
                            if e + 1 < NT:
                                row_max(B, e + 1)
                            if TT <= e < NT + TT:
                                f = e - TT
                                part = (slice(None), (f // TT) % 2, slice(0, i + 1), slice(i * P, (i + 1) * P))
                                v.wait_ge(pt_h_done, B * NT + f + 1)
                                v.tensor_tensor(pt_l[part], bank[TURNS + f % 2][:, 0:width(i)].rearrange("p (j n) -> p j n", n=P),
                                                pt_h[part].bitcast(F32), ALU.subtract).then_inc(pt_done, 1)
                            if i == 1 and u >= 3 and (u - 3) % HG == HG - 1:
                                low_output(B, (u - 3) // HG)
                            if front:
                                if e in STATS:
                                    stat(nxt, STATS.index(e))
                                if e == STATS[-1] + 1:
                                    aggregate(nxt)
                                if e in NORMS:
                                    normalise(nxt, NORMS.index(e))
                                if e in TURNX:
                                    lo_x(nxt, TURNX.index(e))
                                if e - 1 in TURNX:
                                    add_bias(nxt, TURNX.index(e - 1))
                                if e == TURN_KV:
                                    keys(nxt)
                                if e in PROJ_Q:
                                    rotate_q(nxt, PROJ_Q.index(e))
                            if i == 1 and u >= 1 and (u - 1) % HG == HG - 1 and u <= HEADS:
                                hg = (u - 1) // HG
                                v.wait_ge(exp_done, B * NT + u * TT)
                                v.reciprocal(rsum[:, :, :], sums[:, hg % 2]).then_inc(rsum_done, 1)
                                v.wait_ge(rsum_done, B * NHG + hg + 1)
                                v.tensor_copy(rwide[:, :, :, :], rsum[:, :, :].rearrange("p h t -> p t h").unsqueeze(3)
                                              .to_broadcast([P, TT, HG, HD])).then_inc(rwide_done, 1)
                            if i == TT - 1 and u >= 2 and (u - 2) % HG == HG - 1:
                                hg = (u - 2) // HG
                                v.wait_ge(pv_done, B * HEADS + u - 1)
                                v.wait_ge(rt_done, B * NHG + hg + 1)
                                v.tensor_tensor(att, bank[OUTS + hg % 2][:, :], rt, ALU.mult).then_inc(att_done, 1)
                        low_output(B, NHG - 1)
                        if front:
                            rotate_q(nxt, TT - 1)
                            lo_v(nxt)
                        v.wait_ge(x_biased, B * TT + TT)
                        for t in range(TT):
                            v.wait_ge(proj_done, B * TT + t + 1)
                            v.tensor_tensor(x_of(B, t), x_of(B, t), bank[t][:, :], ALU.add).then_inc(x_summed, 1)

                    v.sem_inc(x_summed, TT)
                    for t in range(TT):
                        stat(0, t)
                    aggregate(0)
                    cut_weights(0, wkv_h, wkv_l, raw_kv)
                    for t in range(TT):
                        normalise(0, t)
                        if t >= 1:
                            lo_x(0, t - 1)
                    lo_x(0, TT - 1)
                    cut_weights(1, wq_h, wq_l, raw_q)
                    v.wait_ge(aw_loaded[2], 16)
                    v.wait_ge(aw_loaded[4], 16)
                    v.wait_ge(aw_done, 1)
                    rotate_q(0, 0)
                    keys(0)
                    for t in range(1, TT):
                        rotate_q(0, t)
                    lo_v(0)
                    for t in range(TT):
                        add_bias(0, t)
                    cut_weights(2, wp_h, wp_l, raw_p)
                    with v.Fori(0, BATCHES - 1) as B:
                        batch(B, True)
                    batch(BATCHES - 1, False)

        with nc.Block() as blk:
            @blk.gpsimd
            def _(g):
                g.memset(halves[:, :], -0.5).then_inc(const_pool, 1)
                for i, t in enumerate((ident, ident_b, mask_b)):
                    g.memset(t[:, :], 0.0).then_inc(const_pool, 1)
                g.wait_ge(const_pool, 4)
                for t in (ident, ident_b):
                    g.affine_select(out=t[:, :], in_=t[:, :], compare_op=ALU.not_equal, fill=1.0, base=0,
                                    pattern=[[-1, P]], channel_multiplier=1).then_inc(const_pool, 1)
                g.affine_select(out=mask_b[:, :], in_=mask_b[:, :], compare_op=ALU.is_ge, fill=MASKED, base=0,
                                pattern=[[-1, P]], channel_multiplier=1).then_inc(const_pool, 1)

        ffn_phase(0, x_in, x_mid[0], 0)
        attention_phase(x_mid[0], x_mid[1], GROUPS * NB)
        ffn_phase(1, x_mid[1], out, GROUPS * NB + BATCHES)


_INS = {}


def kernel(**inputs):
    import numpy as _np
    import concourse.bacc as _bacc
    from concourse import mybir as _mybir
    from concourse.bass_utils import run_bass_kernel_spmd as _run

    x = _np.ascontiguousarray(inputs["L0_attn_hidden_states"])
    B, S, D = x.shape
    I = inputs["L0_ffn_w_gate"].shape[1]
    NR, J = 4, 128
    NCH, K = I // (NR * J), D // 128

    def members(w):
        return _np.asarray(w).reshape(K, 128, NCH, J, NR).transpose(2, 4, 1, 0, 3)

    def by_k(w):
        w = _np.asarray(w).T
        return _np.ascontiguousarray(w.reshape(K, 128, -1).transpose(1, 0, 2))

    HD = inputs["L0_attn_w_kv"].shape[0] // 2
    f = _np.float32
    even = _np.arange(0, HD, 2, dtype=f)
    inv = f(1.0) / _np.power(f(10000.0), even / f(HD)).astype(f)
    t = _np.arange(S, dtype=f)
    ang = _np.concatenate([t[:, None] * inv[None, :]] * 2, axis=-1).astype(f)
    base = (even + f(0.4 * HD)) / f(1.4 * HD)
    sc = _np.power(base[None, :], ((t - S // 2) / f(128))[:, None]).astype(f)
    sc = _np.concatenate([sc, sc], axis=-1)
    sign = _np.concatenate([-_np.ones(HD // 2, f), _np.ones(HD // 2, f)])
    tables = _np.stack([_np.cos(ang) * sc / f(HD), _np.sin(ang) * sc * sign / f(HD),
                        _np.cos(ang) / sc, _np.sin(ang) * sign / sc], axis=1).astype(f)
    tables = _np.ascontiguousarray(tables.reshape(S // 128, 128, 4, HD).transpose(1, 0, 2, 3))

    arrays = {
        "x": x,
        "w_gu": _np.ascontiguousarray(_np.stack([members(inputs["L0_ffn_w_gate"]), members(inputs["L0_ffn_w_up"])], axis=3)),
        "w_d": _np.ascontiguousarray(_np.asarray(inputs["L0_ffn_w_down"]).reshape(NCH, J, NR, D).transpose(0, 2, 1, 3)),
        "w_q": by_k(inputs["L0_attn_w_q"]),
        "w_kv": by_k(inputs["L0_attn_w_kv"]),
        "w_p": by_k(inputs["L0_attn_w_proj"]),
        "b_p": _np.ascontiguousarray(_np.asarray(inputs["L0_attn_b_proj"]).reshape(1, D)),
        "rotary": tables,
    }
    nc = _bacc.Bacc("TRN2", target_bir_lowering=False, num_devices=1)
    args = [nc.dram_tensor(f"in_{n}", a.shape, _mybir.dt.from_np(a.dtype), kind="ExternalInput").ap()
            for n, a in arrays.items()]
    args.append(nc.dram_tensor("out_0", x.shape, _mybir.dt.from_np(x.dtype), kind="ExternalOutput").ap())
    macaron_kernel(nc, *args)
    r = _run(nc, [{f"in_{n}": a for n, a in arrays.items()}], core_ids=[0])
    return r.results[0]["out_0"]
```

```python
from contextlib import ExitStack

import concourse.bass as bass
from concourse import mybir

F32 = mybir.dt.float32
F32R = mybir.dt.float32r
BF16 = mybir.dt.bfloat16
ALU = mybir.AluOpType
ACT = mybir.ActivationFunctionType
AX = mybir.AxisListType

P = 128
EPS = 1e-5
MASKED = -3.0e38


def macaron_kernel(nc, x_in, w_gu, w_d, w_q, w_kv, w_p, b_p, rotary, out):
    BATCHES, S, D = x_in.shape
    KD = D // P
    NCH, NR = w_gu.shape[0], w_gu.shape[1]
    TT = S // P
    NB = 2
    GROUPS = BATCHES // NB
    STEPS = NCH * NB
    HD = w_kv.shape[2] // 2
    HEADS = D // HD
    HG = P // HD
    NHG = HEADS // HG
    assert TT == KD == NR == NHG == HG == 4

    x_mid = [nc.dram_tensor(f"x_mid{i}", [BATCHES, S, D], F32, kind="Internal").ap() for i in range(2)]

    def tiles(ap):
        return ap.rearrange("b (t p) d -> b p t d", p=P)

    at = [(nc.sbuf_base + 63) // 64 * 64]

    def place(name, shape, dt):
        size = 1
        for s in shape[1:]:
            size *= s
        size *= 2 if dt == BF16 else 4
        t = nc.alloc_sbuf_tensor_at(name, shape, dt, offset=at[0])
        at[0] += (size + 31) // 32 * 32
        return t

    ident = place("ident", [P, P], F32)
    ident_b = place("ident_b", [P, P], BF16)
    mask_b = place("mask_b", [P, P], BF16)
    halves = place("halves", [P, TT], F32)
    x_sb = place("x_sb", [P, 2, NB * TT, D], F32)
    xnt_h = place("xnt_h", [P, NB, KD, S], F32R)
    xnt_l = place("xnt_l", [P, NB, KD, S], F32R)
    xn = place("xn", [P, 2, D], F32)
    stats = place("stats", [P, NB, TT, 6], F32)
    meanvar = place("meanvar", [P, NB, TT, 2], F32)
    var_eps = place("var_eps", [P, TT], F32)
    rstd = place("rstd", [P, NB, TT], F32)
    shared_end = at[0]

    wgu_h = place("wgu_h", [P, NR, 2, KD, P], F32R)
    wgu_l = place("wgu_l", [P, NR, 2, KD, P], F32R)
    wd_h = place("wd_h", [P, NR, D], F32R)
    wd_l = place("wd_l", [P, NR, D], F32R)
    raw_gu = place("raw_gu", [P, NR, 2, KD, P], F32)
    raw_d = place("raw_d", [P, NR, D], F32)
    sg = place("sg", [P, 2, S], F32)
    h = place("h", [P, NR, S], F32)
    mag = place("mag", [P, NR, S], F32)
    pmax = place("pmax", [P, 2, S], F32)
    first = place("first", [P, 2, S], BF16)
    kept_k = place("kept_k", [P, 2, S], BF16)
    kept_a = place("kept_a", [P, S], BF16)
    ksum = place("ksum", [P, 2, S], BF16)
    kdif = place("kdif", [P, 2, S], BF16)
    hs_h = place("hs_h", [P, NB, NR, S], F32R)
    hs_l = place("hs_l", [P, NB, NR, S], F32R)
    ffn_end = at[0]

    at[0] = shared_end
    wq_h = place("wq_h", [P, KD, D], F32R)
    wq_l = place("wq_l", [P, KD, D], F32R)
    wp_h = place("wp_h", [P, KD, D], F32R)
    wp_l = place("wp_l", [P, KD, D], F32R)
    wkv_h = place("wkv_h", [P, KD, 2 * HD], F32R)
    wkv_l = place("wkv_l", [P, KD, 2 * HD], F32R)
    rot = place("rot", [P, TT, 4, HD], F32)
    bias = place("bias", [P, D], F32)
    kvt = place("kvt", [2 * HD, S], F32)
    kvtok = place("kvtok", [P, TT, 2, HD], F32)
    krot = place("krot", [P, 2, TT, HD], F32)
    kstack = place("kstack", [P, TT, P], F32)
    kt = place("kt", [P, S], F32R)
    VW = 2 * (P - HD) + HD
    v_h = place("v_h", [P, TT, VW], F32R)
    v_l = place("v_l", [P, TT, VW], F32R)
    qrot = place("qrot", [P, TT, D], F32)
    qstack = place("qstack", [P, TT, HG, P], F32)
    qt = place("qt", [P, HG, S], F32R)
    nmax = place("nmax", [P, 2, TT], F32)
    sums = place("sums", [P, 2, HG, TT], F32)
    rsum = place("rsum", [P, HG, TT], F32)
    probs = place("probs", [P, 2, TT, S], F32)
    pt_h = place("pt_h", [P, 2, TT, S], F32R)
    pt_l = place("pt_l", [P, 2, TT, S], F32R)
    rwide = place("rwide", [P, TT, HG, HD], F32)
    att_end = at[0]
    assert max(ffn_end, att_end) <= nc.sbuf_usable_end, (ffn_end, att_end, nc.sbuf_usable_end)
    raw_q, raw_p = probs[:, 0], probs[:, 1]
    raw_kv = qrot[:, 0, 0:KD * 2 * HD].rearrange("p (k n) -> p k n", k=KD)
    att_h, att_l = xnt_h[:, 1], xnt_l[:, 1]
    rt, att, qtmp = x_sb[:, 0, TT], x_sb[:, 0, TT + 1], x_sb[:, 0, TT + 2]

    with ExitStack() as ctx:
        def sem(name):
            return ctx.enter_context(nc.semaphore(name))

        def sems(name, n):
            return [sem(f"{name}{i}") for i in range(n)]

        bank = [ctx.enter_context(nc.psum_tensor(f"bank{i}", [P, 512], F32)) for i in range(8)]

        const_pool = sem("const_pool")
        passed_vector, passed_gpsimd, passed_tensor = sem("passed_vector"), sem("passed_gpsimd"), sem("passed_tensor")
        x_loaded = sems("x_loaded", NB * TT)
        x_stored = sem("x_stored")
        gu_loaded = sems("gu_loaded", NR)
        d_loaded = sems("d_loaded", NR)
        ln_stat = sem("ln_stat")
        rstd_step = sem("rstd_step")
        xn_done = sem("xn_done")
        xn_turned = sem("xn_turned")
        xnt_h_done = sem("xnt_h_done")
        xnt_done = sem("xnt_done")
        wgu_h_done = sem("wgu_h_done")
        wgu_done = sem("wgu_done")
        wd_h_done = sem("wd_h_done")
        wd_done = sem("wd_done")
        gate_done = sem("gate_done")
        up_done = sem("up_done")
        silu_done = sem("silu_done")
        h_done = sem("h_done")
        mag_done = sem("mag_done")
        rank_step = sem("rank_step")
        pruned = sem("pruned")
        hs_h_done = sem("hs_h_done")
        hs_done = sem("hs_done")
        down_done = sem("down_done")
        added = sem("added")
        RANK = 8
        aw_loaded = sems("aw_loaded", 5)
        aw_h_done = sem("aw_h_done")
        aw_done = sem("aw_done")
        pad_done = sem("pad_done")
        ax_loaded = sem("ax_loaded")
        kv_done = sem("kv_done")
        kvt_done = sem("kvt_done")
        kv_turned = sem("kv_turned")
        kvtok_done = sem("kvtok_done")
        k_step = sem("k_step")
        v_h_done = sem("v_h_done")
        v_done = sem("v_done")
        k_turned = sem("k_turned")
        kt_done = sem("kt_done")
        q_done = sem("q_done")
        q_step = sem("q_step")
        stack_h = sem("stack_h")
        stack_done = sem("stack_done")
        stack_turned = sem("stack_turned")
        qt_done = sem("qt_done")
        score_done = sem("score_done")
        max_done = sem("max_done")
        exp_done = sem("exp_done")
        p_turned = sem("p_turned")
        pt_h_done = sem("pt_h_done")
        pt_done = sem("pt_done")
        pv_done = sem("pv_done")
        rsum_done = sem("rsum_done")
        rwide_done = sem("rwide_done")
        r_turned = sem("r_turned")
        rt_done = sem("rt_done")
        att_done = sem("att_done")
        att_h_done = sem("att_h_done")
        att_l_done = sem("att_l_done")
        proj_done = sem("proj_done")
        x_biased = sem("x_biased")
        x_summed = sem("x_summed")
        ax_stored = sem("ax_stored")

        def passed(engine, mark):
            engine.sem_inc(mark, 1)

        def ln_stat_tile(v, slot, t, x):
            v.bn_stats(stats[:, slot, t], x).then_inc(ln_stat, 1)

        def ln_aggregate(v, m, slot):
            v.wait_ge(ln_stat, m * 2 * TT + TT)
            passed(v, passed_vector)
            for t in range(TT):
                v.bn_aggr(meanvar[:, slot, t], stats[:, slot, t]).then_inc(ln_stat, 1)

        def ln_normalise(v, m, slot, t, x):
            if t == 0:
                v.wait_ge(ln_stat, m * 2 * TT + 2 * TT)
                v.wait_ge(rstd_step, m * 2 + 2)
            v.wait_ge(xn_turned, m * TT + t + 1)
            v.tensor_scalar(xn[:, t % 2], x, meanvar[:, slot, t, 0:1], rstd[:, slot, t:t + 1],
                            ALU.subtract, ALU.mult).then_inc(xn_done, 1)

        def ln_lo(v, m, slot, t, ps):
            tok = slice(t * P, (t + 1) * P)
            v.wait_ge(xnt_h_done, m * TT + t + 1)
            v.tensor_tensor(xnt_l[:, slot, :, tok], ps[:, :].rearrange("p (k n) -> p k n", k=KD),
                            xnt_h[:, slot, :, tok].bitcast(F32), ALU.subtract).then_inc(xnt_done, 1)

        def ln_hi(a, m, slot, t, ps):
            a.wait_ge(xn_turned, m * TT + t + 3)
            a.copy(xnt_h[:, slot, :, t * P:(t + 1) * P],
                   ps[:, :].rearrange("p (k n) -> p k n", k=KD)).then_inc(xnt_h_done, 1)

        def ln_turn(pe, m, t, ps):
            pe.wait_ge(xn_done, m * TT + t + 1)
            for k in range(KD):
                last = pe.transpose(ps[:, k * P:(k + 1) * P], xn[:, t % 2, k * P:(k + 1) * P], ident[:, :])
            last.then_inc(xn_turned, 1)

        def ln_gpsimd(g, m, slot):
            g.wait_ge(ln_stat, m * 2 * TT + 2 * TT)
            passed(g, passed_gpsimd)
            g.tensor_scalar(var_eps[:, :], meanvar[:, slot, :, 1], EPS, None, ALU.add).then_inc(rstd_step, 1)
            g.wait_ge(rstd_step, m * 2 + 1)
            g.tensor_tensor(rstd[:, slot], var_eps[:, :], halves[:, :], ALU.pow).then_inc(rstd_step, 1)

        def ffn_phase(phase, src, dst, m0, load_next=None):
            n0 = phase * GROUPS * STEPS
            c0 = phase * GROUPS * NCH
            g0 = phase * GROUPS
            src_t, dst_t = tiles(src), tiles(dst)
            GATE, UP, DOWN = 0, 2, 4
            AFTER = ((0,), (1,), (2, 3), ())

            with nc.Block() as blk:
                @blk.sync
                def _(sp):
                    def load_gu(chunk, c, first=False):
                        for r in range(NR):
                            if not first:
                                sp.wait_ge(wgu_done, (chunk - 1) * NR + r + 1)
                            sp.dma_start(raw_gu[:, r], w_gu[c, r]).then_inc(gu_loaded[r], 16)

                    def load_d(chunk, c, first=False):
                        for r in range(NR):
                            if not first:
                                sp.wait_ge(wd_done, (chunk - 1) * NR + r + 1)
                            sp.dma_start(raw_d[:, r], w_d[c, r]).then_inc(d_loaded[r], 16)

                    def load_x(g, par, blocks=range(NB)):
                        for b in blocks:
                            for t in range(TT):
                                sp.dma_start(x_sb[:, par, b * TT + t], src_t[g * NB + b, :, t]).then_inc(x_loaded[b * TT + t], 16)

                    def store_x(g):
                        for b in range(NB):
                            for t in range(TT):
                                sp.wait_ge(added, (n0 + g * STEPS + STEPS - NB + b) * TT + t + 1 + TT)
                                sp.dma_start(dst_t[g * NB + b, :, t], x_sb[:, g % 2, b * TT + t]).then_inc(x_stored, 16)

                    def group(g, last):
                        with sp.Fori(1, NCH) as c:
                            load_gu(g * NCH + c + c0, c)
                            load_d(g * NCH + c + c0, c)
                        if not last:
                            load_gu((g + 1) * NCH + c0, 0)
                            load_d((g + 1) * NCH + c0, 0)
                        store_x(g)

                    if phase == 0:
                        load_x(0, 0, [0])
                    load_gu(c0, 0, first=True)
                    load_x(0, 0, [1])
                    load_d(c0, 0, first=True)
                    for s in x_loaded:
                        sp.wait_ge(s, (g0 + 1) * 16)
                    load_x(1, 1)
                    group(0, False)
                    with sp.Fori(1, GROUPS - 1) as g:
                        sp.wait_ge(x_stored, (g + g0) * NB * TT * 16)
                        load_x(g + 1, (g + 1) % 2)
                        group(g, False)
                    if load_next is not None:
                        sp.wait_ge(x_stored, (g0 + GROUPS - 1) * NB * TT * 16)
                        load_next(sp)
                    group(GROUPS - 1, True)
                    sp.wait_ge(x_stored, (g0 + GROUPS) * NB * TT * 16)

                @blk.gpsimd
                def _(g):
                    with g.Fori(0, GROUPS) as i:
                        for b in range(NB):
                            ln_gpsimd(g, i * NB + (m0 + b), b)

                @blk.tensor
                def _(pe):
                    def gate_up(n, b, chunk, between=None):
                        for r in range(NR):
                            if b == 0:
                                pe.wait_ge(wgu_done, chunk * NR + r + 1)
                            for kind, done, free, banks in ((0, gate_done, silu_done, GATE), (1, up_done, h_done, UP)):
                                pe.wait_ge(free, n * NR + r + 1)
                                ps = bank[banks + r % 2][:, :]
                                i = 0
                                for k in range(KD):
                                    for w, xs in ((wgu_h, xnt_h), (wgu_h, xnt_l), (wgu_l, xnt_h)):
                                        last = pe.matmul(ps, w[:, r, kind, k], xs[:, b, k], start=(i == 0),
                                                         stop=(i == 3 * KD - 1))
                                        i += 1
                                last.then_inc(done, 1)
                            if between:
                                between(r)

                    def down(n, b, chunk, turned=None):
                        pe.wait_ge(hs_done, n * NR + 2 * NR)
                        if b == 0:
                            pe.wait_ge(wd_done, chunk * NR + NR)
                        for t in range(TT):
                            if turned is not None:
                                pe.wait_ge(xnt_done, turned + t + 1)
                            pe.wait_ge(added, n * TT + t + 1)
                            tok = slice(t * P, (t + 1) * P)
                            i = 0
                            for r in range(NR):
                                for hs, w in ((hs_h, wd_h), (hs_h, wd_l), (hs_l, wd_h)):
                                    last = pe.matmul(bank[DOWN + t][:, :], hs[:, b, r, tok], w[:, r], start=(i == 0),
                                                     stop=(i == 3 * NR - 1))
                                    i += 1
                            last.then_inc(down_done, 1)

                    def group(g, last, first=False):
                        n = g * STEPS + n0
                        m = g * NB + m0
                        chunk = g * NCH + c0
                        if first:
                            pe.wait_ge(xnt_done, m * TT + TT)

                            def turn_other(t):
                                pe.wait_ge(xnt_done, m * TT + t + 1)
                                ln_turn(pe, m + 1, t, bank[DOWN + t])

                            gate_up(n, 0, chunk, lambda r: [turn_other(t) for t in AFTER[r]])
                            pe.wait_ge(xnt_done, m * TT + 2 * TT)
                        else:
                            pe.wait_ge(xnt_done, m * TT + 2 * TT)
                            gate_up(n, 0, chunk)
                        gate_up(n + 1, 1, chunk)
                        down(n, 0, chunk)
                        with pe.Fori(1, NCH - 1) as c:
                            nn = n + c * NB
                            gate_up(nn, 0, chunk + c)
                            down(nn - 1, 1, chunk + c - 1)
                            gate_up(nn + 1, 1, chunk + c)
                            down(nn, 0, chunk + c)
                        nn, end = n + (NCH - 1) * NB, chunk + (NCH - 1)
                        gate_up(nn, 0, end)
                        down(nn - 1, 1, end - 1)
                        if last:
                            gate_up(nn + 1, 1, end)
                            down(nn, 0, end)
                            down(nn + 1, 1, end)
                            return

                        def turn_first(t):
                            pe.wait_ge(added, (nn - 1) * TT + t + 1 + TT)
                            ln_turn(pe, m + NB, t, bank[DOWN + t])

                        def turn_second(t):
                            pe.wait_ge(silu_done if t < UP else h_done, (nn + 1) * NR + NR + 2)
                            ln_turn(pe, m + NB + 1, t, bank[t])

                        gate_up(nn + 1, 1, end, lambda r: [turn_first(t) for t in AFTER[r]])
                        turn_second(0)
                        turn_second(1)
                        down(nn, 0, end, turned=(m + NB) * TT)
                        turn_second(2)
                        turn_second(3)
                        down(nn + 1, 1, end)

                    if phase == 0:
                        pe.sem_inc(xn_turned, 2)
                        pe.sem_inc(down_done, TT)
                        pe.wait_ge(const_pool, 7)
                    for t in range(TT):
                        ln_turn(pe, m0, t, bank[DOWN + t])
                    group(0, False, first=True)
                    with pe.Fori(1, GROUPS - 1) as g:
                        group(g, False)
                    group(GROUPS - 1, True)

                @blk.scalar
                def _(a):
                    def cut_gu(chunk, r):
                        a.wait_ge(gu_loaded[r], chunk * 16 + 16)
                        a.copy(wgu_h[:, r], raw_gu[:, r]).then_inc(wgu_h_done, 1)

                    def step(n, b, chunk, ahead, between=None):
                        for r in range(NR):
                            if b == 1:
                                if r == 0:
                                    a.wait_ge(down_done, n * TT)
                                a.wait_ge(d_loaded[r], chunk * 16 + 16)
                                a.copy(wd_h[:, r], raw_d[:, r]).then_inc(wd_h_done, 1)
                            a.wait_ge(gate_done, n * NR + r + 1)
                            a.wait_ge(h_done, n * NR + r + 1)
                            a.activation(sg[:, r % 2], bank[GATE + r % 2][:, :], ACT.Silu).then_inc(silu_done, 1)
                            if ahead and r >= 1:
                                cut_gu(chunk + 1, r - 1)
                            a.wait_ge(h_done, n * NR + r + 3)
                            a.activation(mag[:, r], h[:, r], ACT.Abs).then_inc(mag_done, 1)
                            if between:
                                between(r)
                        if ahead:
                            a.wait_ge(up_done, n * NR + NR)
                            cut_gu(chunk + 1, NR - 1)
                        for r in range(NR):
                            a.wait_ge(pruned, n * NR + r + 1)
                            a.copy(hs_h[:, b, r], h[:, r]).then_inc(hs_h_done, 1)

                    def group(g, last, first=False):
                        n = g * STEPS + n0
                        m = g * NB + m0
                        chunk = g * NCH + c0
                        if first:
                            step(n, 0, chunk, False, lambda r: [ln_hi(a, m + 1, 1, t, bank[DOWN + t]) for t in AFTER[r]])
                            step(n + 1, 1, chunk, True)
                        with a.Fori(1 if first else 0, NCH - 1) as c:
                            step(n + c * NB, 0, chunk + c, False)
                            step(n + c * NB + 1, 1, chunk + c, True)
                        nn, end = n + (NCH - 1) * NB, chunk + (NCH - 1)
                        step(nn, 0, end, False)
                        if last:
                            step(nn + 1, 1, end, False)
                            return
                        step(nn + 1, 1, end, True, lambda r: [ln_hi(a, m + NB, 0, t, bank[DOWN + t]) for t in AFTER[r]])
                        for t in range(TT):
                            ln_hi(a, m + NB + 1, 1, t, bank[t])

                    if phase == 0:
                        a.sem_inc(silu_done, 2)
                    for t in range(TT):
                        ln_hi(a, m0, 0, t, bank[DOWN + t])
                    for r in range(NR):
                        cut_gu(c0, r)
                    group(0, False, first=True)
                    with a.Fori(1, GROUPS - 1) as g:
                        group(g, False)
                    group(GROUPS - 1, True)

                @blk.vector
                def _(v):
                    def cut_gu(chunk, r):
                        v.wait_ge(wgu_h_done, chunk * NR + r + 1)
                        v.tensor_tensor(wgu_l[:, r], raw_gu[:, r], wgu_h[:, r].bitcast(F32),
                                        ALU.subtract).then_inc(wgu_done, 1)

                    def add_down(n, b, par):
                        for t in range(TT):
                            v.wait_ge(down_done, n * TT + t + 1 + TT)
                            x = x_sb[:, par, b * TT + t]
                            v.scalar_tensor_tensor(out=x, in0=bank[DOWN + t][:, :], scalar=0.5, in1=x, op0=ALU.mult,
                                                   op1=ALU.add).then_inc(added, 1)

                    def hidden(n, b, chunk, ahead, between=None):
                        v.wait_ge(hs_done, n * NR + NR)
                        for r in range(NR):
                            if b == 1:
                                v.wait_ge(wd_h_done, chunk * NR + r + 1)
                                v.tensor_tensor(wd_l[:, r], raw_d[:, r], wd_h[:, r].bitcast(F32),
                                                ALU.subtract).then_inc(wd_done, 1)
                            v.wait_ge(up_done, n * NR + r + 1)
                            v.wait_ge(silu_done, n * NR + r + 3)
                            v.tensor_tensor(h[:, r], bank[UP + r % 2][:, :], sg[:, r % 2], ALU.mult).then_inc(h_done, 1)
                            if ahead and r >= 1:
                                cut_gu(chunk + 1, r - 1)
                            if between:
                                between(r)

                    def prune(n):
                        pair = mag[:, :, :].rearrange("p (a e) s -> p a e s", e=2)
                        base = n * RANK
                        v.wait_ge(mag_done, n * NR + NR)
                        v.tensor_tensor(first[:, :, :], pair[:, :, 0], pair[:, :, 1], ALU.is_ge).then_inc(rank_step, 1)
                        v.tensor_tensor(pmax[:, :, :], pair[:, :, 0], pair[:, :, 1], ALU.max).then_inc(rank_step, 1)
                        v.tensor_tensor(pair[:, :, 0], pair[:, :, 0], pair[:, :, 1], ALU.min).then_inc(rank_step, 1)
                        v.wait_ge(rank_step, base + 3)
                        v.tensor_tensor(kept_k[:, 0], mag[:, 0], pmax[:, 1], ALU.is_ge).then_inc(rank_step, 1)
                        v.tensor_tensor(kept_k[:, 1], pmax[:, 0], mag[:, 2], ALU.is_ge).then_inc(rank_step, 1)
                        v.wait_ge(rank_step, base + 5)
                        v.tensor_tensor(kept_a[:, :], kept_k[:, 0], kept_k[:, 1], ALU.add).then_inc(rank_step, 1)
                        v.wait_ge(rank_step, base + 6)
                        wide = kept_a[:, :].unsqueeze(1).to_broadcast([P, 2, S])
                        v.tensor_tensor(ksum[:, :, :], wide, first[:, :, :], ALU.add).then_inc(rank_step, 1)
                        v.tensor_tensor(kdif[:, :, :], wide, first[:, :, :], ALU.subtract).then_inc(rank_step, 1)
                        v.wait_ge(rank_step, base + 8)
                        rules = ((ksum[:, 0], 2.0, ALU.is_ge), (kdif[:, 0], 1.0, ALU.is_ge),
                                 (kdif[:, 1], 0.0, ALU.is_le), (ksum[:, 1], 1.0, ALU.is_le))
                        for r, (count, least, op) in enumerate(rules):
                            v.scalar_tensor_tensor(out=h[:, r], in0=count, scalar=least, in1=h[:, r], op0=op,
                                                   op1=ALU.mult).then_inc(pruned, 1)

                    def cut_hidden(n, b):
                        for r in range(NR):
                            v.wait_ge(hs_h_done, n * NR + r + 1)
                            v.tensor_tensor(hs_l[:, b, r], h[:, r], hs_h[:, b, r].bitcast(F32),
                                            ALU.subtract).then_inc(hs_done, 1)

                    def step(n, b, chunk, ahead, before, par):
                        hidden(n, b, chunk, ahead)
                        if ahead:
                            cut_gu(chunk + 1, NR - 1)
                        prune(n)
                        if before:
                            add_down(n - 1, 1 - b, par)
                        cut_hidden(n, b)

                    def group(g, par, last, first=False):
                        n = g * STEPS + n0
                        m = g * NB + m0
                        chunk = g * NCH + c0
                        if first:
                            def other_block(r):
                                for t in AFTER[r]:
                                    ln_lo(v, m + 1, 1, t, bank[DOWN + t])
                                    if t + 2 < TT:
                                        ln_normalise(v, m + 1, 1, t + 2, x_sb[:, par, TT + t + 2])

                            hidden(n, 0, chunk, False, other_block)
                            prune(n)
                            cut_hidden(n, 0)
                        else:
                            step(n, 0, chunk, False, False, par)
                        step(n + 1, 1, chunk, True, True, par)
                        with v.Fori(1, NCH - 1) as c:
                            step(n + c * NB, 0, chunk + c, False, True, par)
                            step(n + c * NB + 1, 1, chunk + c, True, True, par)
                        nn, end = n + (NCH - 1) * NB, chunk + (NCH - 1)
                        if last:
                            step(nn, 0, end, False, True, par)
                            step(nn + 1, 1, end, False, True, par)
                            add_down(nn + 1, 1, par)
                            return
                        nxt = (g + 1) % 2

                        def x_next(b, t):
                            return x_sb[:, nxt, b * TT + t]

                        for t in range(TT):
                            v.wait_ge(x_loaded[t], (g + (g0 + 2)) * 16)
                            ln_stat_tile(v, 0, t, x_next(0, t))
                        ln_aggregate(v, m + NB, 0)
                        step(nn, 0, end, False, True, par)
                        ln_normalise(v, m + NB, 0, 0, x_next(0, 0))
                        ln_normalise(v, m + NB, 0, 1, x_next(0, 1))
                        for t in range(TT):
                            v.wait_ge(x_loaded[TT + t], (g + (g0 + 2)) * 16)
                            ln_stat_tile(v, 1, t, x_next(1, t))
                        ln_aggregate(v, m + NB + 1, 1)

                        def first_block(r):
                            for t in AFTER[r]:
                                ln_lo(v, m + NB, 0, t, bank[DOWN + t])
                                if t + 2 < TT:
                                    ln_normalise(v, m + NB, 0, t + 2, x_next(0, t + 2))
                            if AFTER[r] and AFTER[r][-1] == TT - 1:
                                ln_normalise(v, m + NB + 1, 1, 0, x_next(1, 0))
                                ln_normalise(v, m + NB + 1, 1, 1, x_next(1, 1))

                        hidden(nn + 1, 1, end, True, first_block)
                        prune(nn + 1)
                        ln_normalise(v, m + NB + 1, 1, 2, x_next(1, 2))
                        ln_normalise(v, m + NB + 1, 1, 3, x_next(1, 3))
                        cut_hidden(nn + 1, 1)
                        add_down(nn, 0, par)
                        for t in range(TT):
                            ln_lo(v, m + NB + 1, 1, t, bank[t])
                        cut_gu(end + 1, NR - 1)
                        add_down(nn + 1, 1, par)

                    if phase == 0:
                        v.sem_inc(h_done, 2)
                        v.sem_inc(hs_done, NR)
                        v.sem_inc(added, TT)
                    def first_stat(b, t):
                        v.wait_ge(x_loaded[b * TT + t], g0 * 16 + 16)
                        ln_stat_tile(v, b, t, x_sb[:, 0, b * TT + t])

                    for t in range(TT):
                        first_stat(0, t)
                    ln_aggregate(v, m0, 0)
                    for t in range(TT + 1):
                        if t < TT:
                            ln_normalise(v, m0, 0, t, x_sb[:, 0, t])
                        if t >= 1:
                            ln_lo(v, m0, 0, t - 1, bank[DOWN + t - 1])
                            first_stat(1, t - 1)
                    ln_aggregate(v, m0 + 1, 1)
                    for r in range(NR):
                        cut_gu(c0, r)
                        if r < 2:
                            ln_normalise(v, m0 + 1, 1, r, x_sb[:, 0, TT + r])
                    group(0, 0, False, first=True)
                    with v.Fori(1, GROUPS - 1) as g:
                        group(g, g % 2, False)
                    group(GROUPS - 1, (GROUPS - 1) % 2, True)

        def attention_phase(src, dst, m0):
            src_t, dst_t = tiles(src), tiles(dst)
            NT = HEADS * TT
            SCORES, TURNS, OUTS, SPARE = 0, 3, 5, 7
            KSTEP, QSTEP = 6, 4
            HALF = HD // 2
            meets = [(j * P if j < TT - 1 else (TT - 2) * P) for j in range(TT)]
            STATS = [(4 + t) * TT + 2 for t in range(TT)]
            NORMS = [(8 + t) * TT + 2 for t in range(TT)]
            TURNX = [(9 + t) * TT + 1 for t in range(TT)]
            PROJ_KV, TURN_KV = 13 * TT + 1, 14 * TT + 1
            PROJ_Q = [14 * TT + 3, 15 * TT + 3, 16 * TT + 3]
            TURN_K = 16 * TT

            def width(i):
                return (i + 1) * P

            def heads_of(ap):
                return ap.rearrange("p (h d) -> p h d", d=HD)

            spare = bank[SPARE]

            with nc.Block() as blk:
                @blk.sync
                def _(sp):
                    sp.dma_start(raw_kv, w_kv).then_inc(aw_loaded[0], 16)
                    sp.dma_start(raw_q, w_q).then_inc(aw_loaded[1], 16)
                    sp.dma_start(rot[:, :, :, :], rotary).then_inc(aw_loaded[2], 16)
                    sp.dma_start(raw_p, w_p).then_inc(aw_loaded[3], 16)
                    sp.dma_start(bias[:, :], b_p.to_broadcast([P, D])).then_inc(aw_loaded[4], 16)
                    sp.wait_ge(ax_loaded, 16)
                    sp.dma_start(x_sb[:, 1, 0:TT], src_t[1]).then_inc(ax_loaded, 16)

                    def store(B, par):
                        for t in range(TT):
                            sp.wait_ge(x_summed, B * TT + t + 1 + TT)
                            sp.dma_start(dst_t[B, :, t], x_sb[:, par, t]).then_inc(ax_stored, 16)

                    with sp.Fori(0, BATCHES - 2) as B:
                        store(B, B % 2)
                        sp.wait_ge(ax_stored, (B * TT + TT) * 16)
                        sp.wait_ge(ax_loaded, (B + 2) * 16)
                        sp.dma_start(x_sb[:, B % 2, 0:TT], src_t[B + 2]).then_inc(ax_loaded, 16)
                    store(BATCHES - 2, (BATCHES - 2) % 2)
                    sp.wait_ge(ax_stored, (BATCHES - 1) * TT * 16)
                    for t in range(TT):
                        sp.dma_start(x_sb[:, 0, t], dst_t[0, :, t]).then_inc(x_loaded[t], 16)
                    store(BATCHES - 1, (BATCHES - 1) % 2)
                    sp.wait_ge(ax_stored, BATCHES * TT * 16)

                @blk.gpsimd
                def _(g):
                    def stack_head(B, w):
                        if w == 0:
                            g.wait_ge(q_step, (B + 1) * QSTEP * TT)
                            passed(g, passed_gpsimd)
                        g.wait_ge(stack_turned, B * HEADS + w + 1)
                        passed(g, passed_gpsimd)
                        slot = qstack[:, :, w % HG].rearrange("p t (e c d) -> p t e c d", e=2, c=2)
                        q = qrot[:, :, w * HD:(w + 1) * HD].unsqueeze(2).to_broadcast([P, TT, 2, HD])
                        g.tensor_copy(slot[:, :, :, 0].bitcast(F32R), q).then_inc(stack_h, 1)
                        g.wait_ge(stack_h, B * HEADS + w + 1)
                        g.tensor_tensor(slot[:, :, :, 1], q, slot[:, :, :, 0], ALU.subtract).then_inc(stack_done, 1)

                    def add_bias(B, t):
                        g.wait_ge(xn_done, (B + m0) * TT + t + 1)
                        passed(g, passed_gpsimd)
                        x = x_sb[:, B % 2, t]
                        g.tensor_tensor(x, x, bias[:, :], ALU.add).then_inc(x_biased, 1)

                    def finish_q(B, t):
                        g.wait_ge(q_step, (B * TT + t) * QSTEP + 3)
                        passed(g, passed_gpsimd)
                        g.tensor_tensor(qrot[:, t], qrot[:, t], qtmp, ALU.add).then_inc(q_step, 1)

                    def batch(B, front):
                        for w in range(2, HEADS):
                            stack_head(B, w)
                            if front and w == HEADS - 3:
                                ln_gpsimd(g, B + (m0 + 1), 0)
                        if front:
                            for t in range(TT):
                                add_bias(B + 1, t)
                            for t in range(TT - 1):
                                finish_q(B + 1, t)
                            stack_head(B + 1, 0)
                            stack_head(B + 1, 1)

                    g.sem_inc(stack_done, HEADS)
                    ln_gpsimd(g, m0, 0)
                    for t in (v_h, v_l):
                        g.memset(t[:, :, :].bitcast(F32), 0.0).then_inc(pad_done, 1)
                    for t in (pt_h, pt_l):
                        g.memset(t[:, :, TT - 1, meets[-1]:(TT - 1) * P].bitcast(F32), 0.0).then_inc(pad_done, 1)
                    stack_head(0, 0)
                    stack_head(0, 1)
                    with g.Fori(0, BATCHES - 1) as B:
                        batch(B, True)
                    batch(BATCHES - 1, False)

                @blk.tensor
                def _(pe):
                    class Spare:
                        sem, value = None, None

                    def take_spare(drained_by, value):
                        if Spare.sem is not None:
                            pe.wait_ge(Spare.sem, Spare.value)
                        Spare.sem, Spare.value = drained_by, value

                    def project_x(ps, w_hi, w_lo, t=None, ks=range(KD)):
                        i = 3 * ks[0]
                        for k in ks:
                            for a, b in ((w_hi, xnt_h), (w_lo, xnt_h), (w_hi, xnt_l)):
                                x = b[:, 0, k] if t is None else b[:, 0, k, t * P:(t + 1) * P]
                                still, moving = (a[:, k], x) if t is None else (x, a[:, k])
                                last = pe.matmul(ps, still, moving, start=(i == 0), stop=(i == 3 * KD - 1))
                                i += 1
                        return last

                    def turn_x(B, t):
                        take_spare(xnt_done, (B + m0) * TT + t + 1)
                        ln_turn(pe, B + m0, t, spare)

                    def project_kv(B):
                        take_spare(kvt_done, B + 1)
                        project_x(spare[0:2 * HD, :], wkv_h, wkv_l).then_inc(kv_done, 1)

                    def turn_kv(B):
                        take_spare(kvtok_done, B + 1)
                        passed(pe, passed_tensor)
                        for t in range(TT):
                            last = pe.transpose(spare[:, t * 2 * HD:(t + 1) * 2 * HD], kvt[:, t * P:(t + 1) * P],
                                                ident[0:2 * HD, 0:2 * HD])
                        last.then_inc(kv_turned, 1)

                    def turn_k(B):
                        pe.wait_ge(k_step, B * KSTEP + KSTEP)
                        take_spare(kt_done, B + 1)
                        for t in range(TT):
                            last = pe.transpose(spare[:, t * P:(t + 1) * P], kstack[:, t], ident[:, :])
                        last.then_inc(k_turned, 1)

                    def project_q(B, t, half=None):
                        if half != 1:
                            take_spare(q_step, (B * TT + t) * QSTEP + QSTEP - 1)
                        ks = range(KD) if half is None else range(half * KD // 2, (half + 1) * KD // 2)
                        last = project_x(spare[:, :], wq_h, wq_l, t, ks)
                        if half != 0:
                            last.then_inc(q_done, 1)

                    def turn_stack(B, w):
                        pe.wait_ge(stack_done, B * HEADS + w + 1 + HEADS)
                        take_spare(qt_done, B * HEADS + w + 1)
                        for t in range(TT):
                            last = pe.transpose(spare[:, t * P:(t + 1) * P], qstack[:, t, w % HG], ident[:, :])
                        last.then_inc(stack_turned, 1)

                    def turn_sums(B, hg):
                        pe.wait_ge(rwide_done, B * NHG + hg + 1)
                        take_spare(rt_done, B * NHG + hg + 1)
                        for t in range(TT):
                            last = pe.transpose(spare[:, t * P:(t + 1) * P],
                                                rwide[:, t].rearrange("p h d -> p (h d)"), ident[:, :])
                        last.then_inc(r_turned, 1)

                    def scores(B, e):
                        u, i = e // TT, e % TT
                        if e >= 3:
                            pe.wait_ge(exp_done, B * NT + e - 2)
                        else:
                            pe.wait_ge(x_summed, B * TT + e + 1)
                        if e == 0:
                            pe.wait_ge(kt_done, B + 1)
                        if i == 0:
                            pe.wait_ge(qt_done, B * HEADS + u + 1)
                        ps = bank[SCORES + e % 3]
                        n = max(width(i), 2 * P)
                        pe.matmul(ps[:, 0:n], qt[:, u % HG, i * P:(i + 1) * P], kt[:, 0:n], start=True, stop=False)
                        pe.matmul(ps[:, i * P:width(i)], ident_b[:, :], mask_b[:, :], start=False,
                                  stop=True).then_inc(score_done, 1)

                    def turn_probs(B, e):
                        u, i = e // TT, e % TT
                        pe.wait_ge(exp_done, B * NT + e + 1)
                        if e >= 2:
                            pe.wait_ge(pt_done, B * NT + e - 1)
                        else:
                            pe.wait_ge(x_summed, B * TT + TT)
                        for j in range(i + 1):
                            last = pe.transpose(bank[TURNS + e % 2][:, j * P:(j + 1) * P],
                                                probs[:, u % 2, i, j * P:(j + 1) * P], ident[:, :])
                        last.then_inc(p_turned, 1)

                    def weigh(B, e):
                        u, j = e // TT, e % TT
                        hg, s = u // HG, u % HG
                        if e == 0:
                            pe.wait_ge(v_done, B + 1)
                        if j == 0:
                            pe.wait_ge(pt_done, B * NT + u * TT + TT)
                            if s == 0 and hg >= 2:
                                pe.wait_ge(att_done, B * NHG + hg - 1)
                        window = slice((HG - 1 - s) * HD, (HG - 1 - s) * HD + P)
                        a = meets[j]
                        for i, (v, pt) in enumerate(((v_h, pt_h), (v_l, pt_h), (v_h, pt_l))):
                            last = pe.matmul(bank[OUTS + hg % 2][:, a:S], v[:, j, window], pt[:, u % 2, j, a:S],
                                             start=(s == 0 and j == 0 and i == 0),
                                             stop=(s == HG - 1 and j == TT - 1 and i == 2))
                        if j == TT - 1:
                            last.then_inc(pv_done, 1)

                    def project_out(t):
                        i = 0
                        for k in range(KD):
                            for a, w in ((att_h, wp_h), (att_h, wp_l), (att_l, wp_h)):
                                last = pe.matmul(bank[t][:, :], a[:, k, t * P:(t + 1) * P], w[:, k],
                                                 start=(i == 0), stop=(i == 3 * KD - 1))
                                i += 1
                        last.then_inc(proj_done, 1)

                    def batch(B, front):
                        nxt = B + 1
                        Spare.sem, Spare.value = qt_done, B * HEADS + 2
                        scores(B, 0)
                        for e in range(NT + 2 * TT + 2):
                            u, i = e // TT, e % TT
                            if e + 1 < NT:
                                scores(B, e + 1)
                            if e >= 2 * TT + 2:
                                weigh(B, e - (2 * TT + 2))
                            if TT <= e < NT + TT:
                                turn_probs(B, e - TT)
                            if front:
                                if e in TURNX:
                                    turn_x(nxt, TURNX.index(e))
                                if e == PROJ_KV:
                                    pe.wait_ge(xnt_done, (nxt + m0) * TT + TT)
                                    project_kv(nxt)
                                if e == TURN_KV:
                                    turn_kv(nxt)
                                if e == TURN_K:
                                    turn_k(nxt)
                                if e + 1 in PROJ_Q:
                                    project_q(nxt, PROJ_Q.index(e + 1), 0)
                                if e in PROJ_Q:
                                    project_q(nxt, PROJ_Q.index(e), 1)
                            if i == 0 and u + 2 < HEADS:
                                turn_stack(B, u + 2)
                            if i == 3 and u >= 2 and (u - 2) % HG == HG - 1:
                                turn_sums(B, (u - 2) // HG)
                        if front:
                            project_q(nxt, TT - 1)
                        pe.wait_ge(att_l_done, B * NHG + NHG)
                        for t in range(TT):
                            project_out(t)
                            if front and t >= TT - 2:
                                turn_stack(nxt, t - (TT - 2))

                    pe.sem_inc(stack_turned, HG)
                    for t in range(TT):
                        turn_x(0, t)
                    pe.wait_ge(xnt_done, m0 * TT + TT)
                    pe.wait_ge(aw_done, 1 + KD)
                    project_kv(0)
                    project_q(0, 0)
                    turn_kv(0)
                    project_q(0, 1)
                    project_q(0, 2)
                    turn_k(0)
                    project_q(0, 3)
                    turn_stack(0, 0)
                    turn_stack(0, 1)
                    pe.wait_ge(aw_done, 2 + KD)
                    with pe.Fori(0, BATCHES - 1) as B:
                        batch(B, True)
                    batch(BATCHES - 1, False)

                @blk.scalar
                def _(a):
                    def drain_kv(B):
                        a.wait_ge(kv_done, B + 1)
                        a.copy(kvt[:, :], spare[0:2 * HD, :]).then_inc(kvt_done, 1)

                    def drain_kvtok(B):
                        a.wait_ge(kv_turned, B + 1)
                        a.copy(kvtok[:, :, :, :], spare[:, 0:TT * 2 * HD].rearrange("p (t c d) -> p t c d", t=TT, c=2)
                               ).then_inc(kvtok_done, 1)

                    def drain_k(B):
                        a.wait_ge(k_turned, B + 1)
                        a.copy(kt[:, :], spare[:, :]).then_inc(kt_done, 1)

                    def hi_v(B):
                        a.wait_ge(kvtok_done, B + 1)
                        a.copy(v_h[:, :, P - HD:P], kvtok[:, :, 1]).then_inc(v_h_done, 1)

                    def queries(B, w):
                        a.wait_ge(stack_turned, B * HEADS + w + 1 + HG)
                        a.copy(qt[:, w % HG], spare[:, :]).then_inc(qt_done, 1)

                    def cast_output(B, hg):
                        a.wait_ge(att_done, B * NHG + hg + 1)
                        a.copy(att_h[:, hg], att).then_inc(att_h_done, 1)

                    def batch(B, front):
                        nxt = B + 1
                        for e in range(NT + 2 * TT + 2):
                            u, i = e // TT, e % TT
                            if e < NT:
                                a.wait_ge(max_done, B * NT + e + 1)
                                a.activation(probs[:, u % 2, i, 0:width(i)], bank[SCORES + e % 3][:, 0:width(i)], ACT.Exp,
                                             bias=nmax[:, u % 2, i:i + 1],
                                             accum_out=sums[:, (u // HG) % 2, u % HG, i:i + 1]).then_inc(exp_done, 1)
                            if TT <= e < NT + TT:
                                f = e - TT
                                a.wait_ge(p_turned, B * NT + f + 1)
                                a.copy(pt_h[:, (f // TT) % 2, 0:i + 1, i * P:(i + 1) * P],
                                       bank[TURNS + f % 2][:, 0:width(i)].rearrange("p (j n) -> p j n", n=P)
                                       ).then_inc(pt_h_done, 1)
                            if i == 2 and u >= 3 and (u - 3) % HG == HG - 1:
                                cast_output(B, (u - 3) // HG)
                            if front:
                                if e in TURNX:
                                    ln_hi(a, nxt + m0, 0, TURNX.index(e), spare)
                                if e == PROJ_KV:
                                    drain_kv(nxt)
                                if e == TURN_KV:
                                    drain_kvtok(nxt)
                                if e == TURN_K:
                                    drain_k(nxt)
                            if i == 0 and u + 2 < HEADS:
                                queries(B, u + 2)
                            if i == 3 and u >= 2 and (u - 2) % HG == HG - 1:
                                a.wait_ge(r_turned, B * NHG + (u - 2) // HG + 1)
                                a.copy(rt, spare[:, :]).then_inc(rt_done, 1)
                        cast_output(B, NHG - 1)
                        if front:
                            a.wait_ge(pv_done, B * HEADS + HEADS)
                            hi_v(nxt)
                            queries(nxt, 0)
                            queries(nxt, 1)

                    for i, (ld, hi, raw) in enumerate(((0, wkv_h, raw_kv), (1, wq_h, raw_q))):
                        a.wait_ge(aw_loaded[ld], 16)
                        a.copy(hi[:, :, :], raw).then_inc(aw_h_done, 1)
                    for t in range(TT):
                        ln_hi(a, m0, 0, t, spare)
                    drain_kv(0)
                    drain_kvtok(0)
                    a.wait_ge(pad_done, 4)
                    hi_v(0)
                    drain_k(0)
                    a.wait_ge(aw_loaded[3], 16)
                    a.copy(wp_h[:, :, :], raw_p).then_inc(aw_h_done, 1)
                    queries(0, 0)
                    queries(0, 1)
                    with a.Fori(0, BATCHES - 1) as B:
                        batch(B, True)
                    batch(BATCHES - 1, False)

                @blk.vector
                def _(v):
                    def cut_weights(i, hi, lo, raw, k=None):
                        ks = slice(0, KD) if k is None else slice(k, k + 1)
                        v.wait_ge(aw_h_done, i + 1)
                        v.tensor_tensor(lo[:, ks], raw[:, ks], hi[:, ks].bitcast(F32), ALU.subtract).then_inc(aw_done, 1)

                    def rotate(x, dst, tmp, cos, sin, step, base, finish=True):
                        v.tensor_tensor(dst, x, cos, ALU.mult).then_inc(step, 1)
                        v.tensor_tensor(tmp[:, :, 0:HALF], x[:, :, HALF:HD], sin[:, :, 0:HALF], ALU.mult).then_inc(step, 1)
                        v.tensor_tensor(tmp[:, :, HALF:HD], x[:, :, 0:HALF], sin[:, :, HALF:HD], ALU.mult).then_inc(step, 1)
                        if finish:
                            v.wait_ge(step, base + 3)
                            v.tensor_tensor(dst, dst, tmp, ALU.add).then_inc(step, 1)
                            v.wait_ge(step, base + 4)

                    def x_of(B, t):
                        return x_sb[:, B % 2, t]

                    def stat(B, t):
                        if t == 0:
                            v.wait_ge(ax_loaded, B * 16 + 16)
                        ln_stat_tile(v, 0, t, x_of(B, t))

                    def add_bias(B, t):
                        v.wait_ge(xn_done, (B + m0) * TT + t + 1)
                        v.tensor_tensor(x_of(B, t), x_of(B, t), bias[:, :], ALU.add).then_inc(x_biased, 1)

                    def keys(B):
                        v.wait_ge(kvtok_done, B + 1)
                        rotate(kvtok[:, :, 0], krot[:, 0], krot[:, 1], rot[:, :, 2], rot[:, :, 3], k_step, B * KSTEP)
                        ks = kstack[:, :, :].rearrange("p t (c e d) -> p t c e d", c=2, e=2)
                        kr = krot[:, 0].unsqueeze(2).to_broadcast([P, TT, 2, HD])
                        v.tensor_copy(ks[:, :, 0].bitcast(F32R), kr).then_inc(k_step, 1)
                        v.wait_ge(k_step, B * KSTEP + 5)
                        v.tensor_tensor(ks[:, :, 1], kr, ks[:, :, 0], ALU.subtract).then_inc(k_step, 1)

                    def lo_v(B):
                        v.wait_ge(v_h_done, B + 1)
                        v.tensor_tensor(v_l[:, :, P - HD:P], kvtok[:, :, 1], v_h[:, :, P - HD:P].bitcast(F32),
                                        ALU.subtract).then_inc(v_done, 1)

                    def rotate_q(B, t, finish=True):
                        if t == 0:
                            v.wait_ge(stack_done, B * HEADS + HEADS)
                        v.wait_ge(q_done, B * TT + t + 1)
                        v.wait_ge(q_step, (B * TT + t) * QSTEP)
                        passed(v, passed_vector)
                        cos = rot[:, t, 0].unsqueeze(1).to_broadcast([P, HEADS, HD])
                        sin = rot[:, t, 1].unsqueeze(1).to_broadcast([P, HEADS, HD])
                        rotate(heads_of(spare[:, :]), heads_of(qrot[:, t]), heads_of(qtmp), cos, sin,
                               q_step, (B * TT + t) * QSTEP, finish)

                    def low_output(B, hg):
                        v.wait_ge(att_h_done, B * NHG + hg + 1)
                        v.tensor_tensor(att_l[:, hg], att, att_h[:, hg].bitcast(F32), ALU.subtract).then_inc(att_l_done, 1)

                    def row_max(B, e):
                        u, i = e // TT, e % TT
                        v.wait_ge(score_done, B * NT + e + 1)
                        v.tensor_reduce(nmax[:, u % 2, i:i + 1], bank[SCORES + e % 3][:, 0:width(i)], AX.X, ALU.max,
                                        negate=True).then_inc(max_done, 1)

                    def batch(B, front):
                        nxt = B + 1
                        row_max(B, 0)
                        for e in range(NT + 2 * TT + 2):
                            u, i = e // TT, e % TT
                            if e + 1 < NT:
                                row_max(B, e + 1)
                            if TT <= e < NT + TT:
                                f = e - TT
                                part = (slice(None), (f // TT) % 2, slice(0, i + 1), slice(i * P, (i + 1) * P))
                                v.wait_ge(pt_h_done, B * NT + f + 1)
                                v.tensor_tensor(pt_l[part], bank[TURNS + f % 2][:, 0:width(i)].rearrange("p (j n) -> p j n", n=P),
                                                pt_h[part].bitcast(F32), ALU.subtract).then_inc(pt_done, 1)
                            if i == 0 and u >= 4 and (u - 4) % HG == HG - 1:
                                low_output(B, (u - 4) // HG)
                            if front:
                                if e in STATS:
                                    stat(nxt, STATS.index(e))
                                if e == STATS[-1] + 1:
                                    ln_aggregate(v, nxt + m0, 0)
                                if e in NORMS:
                                    ln_normalise(v, nxt + m0, 0, NORMS.index(e), x_of(nxt, NORMS.index(e)))
                                if e in TURNX:
                                    ln_lo(v, nxt + m0, 0, TURNX.index(e), spare)
                                if e == TURN_KV:
                                    keys(nxt)
                                if e in PROJ_Q:
                                    rotate_q(nxt, PROJ_Q.index(e), finish=False)
                            if i == 0 and u >= 2 and (u - 2) % HG == HG - 1:
                                hg = (u - 2) // HG
                                v.wait_ge(exp_done, B * NT + (u - 1) * TT)
                                v.reciprocal(rsum[:, :, :], sums[:, hg % 2]).then_inc(rsum_done, 1)
                                v.wait_ge(rsum_done, B * NHG + hg + 1)
                                v.tensor_copy(rwide[:, :, :, :], rsum[:, :, :].rearrange("p h t -> p t h").unsqueeze(3)
                                              .to_broadcast([P, TT, HG, HD])).then_inc(rwide_done, 1)
                            if i == 1 and u >= 3 and (u - 3) % HG == HG - 1:
                                hg = (u - 3) // HG
                                v.wait_ge(pv_done, B * HEADS + u - 2)
                                v.wait_ge(rt_done, B * NHG + hg + 1)
                                v.tensor_tensor(att, bank[OUTS + hg % 2][:, :], rt, ALU.mult).then_inc(att_done, 1)
                        low_output(B, NHG - 1)
                        if front:
                            rotate_q(nxt, TT - 1)
                            lo_v(nxt)
                        v.wait_ge(x_biased, B * TT + TT)
                        for t in range(TT):
                            v.wait_ge(proj_done, B * TT + t + 1)
                            v.tensor_tensor(x_of(B, t), x_of(B, t), bank[t][:, :], ALU.add).then_inc(x_summed, 1)

                    v.sem_inc(x_summed, TT)
                    for t in range(TT):
                        stat(0, t)
                    ln_aggregate(v, m0, 0)
                    cut_weights(0, wkv_h, wkv_l, raw_kv)
                    for t in range(TT):
                        ln_normalise(v, m0, 0, t, x_of(0, t))
                        if t >= 1:
                            ln_lo(v, m0, 0, t - 1, spare)
                            cut_weights(1, wq_h, wq_l, raw_q, t - 1)
                    ln_lo(v, m0, 0, TT - 1, spare)
                    cut_weights(1, wq_h, wq_l, raw_q, TT - 1)
                    v.wait_ge(aw_loaded[2], 16)
                    v.wait_ge(aw_loaded[4], 16)
                    v.wait_ge(aw_done, 1)
                    rotate_q(0, 0)
                    keys(0)
                    for t in range(1, TT):
                        rotate_q(0, t)
                    lo_v(0)
                    for t in range(TT):
                        add_bias(0, t)
                    cut_weights(2, wp_h, wp_l, raw_p)
                    with v.Fori(0, BATCHES - 1) as B:
                        batch(B, True)
                    batch(BATCHES - 1, False)

        with nc.Block() as blk:
            @blk.gpsimd
            def _(g):
                g.memset(halves[:, :], -0.5).then_inc(const_pool, 1)
                for i, t in enumerate((ident, ident_b, mask_b)):
                    g.memset(t[:, :], 0.0).then_inc(const_pool, 1)
                g.wait_ge(const_pool, 4)
                for t in (ident, ident_b):
                    g.affine_select(out=t[:, :], in_=t[:, :], compare_op=ALU.not_equal, fill=1.0, base=0,
                                    pattern=[[-1, P]], channel_multiplier=1).then_inc(const_pool, 1)
                g.affine_select(out=mask_b[:, :], in_=mask_b[:, :], compare_op=ALU.is_ge, fill=MASKED, base=0,
                                pattern=[[-1, P]], channel_multiplier=1).then_inc(const_pool, 1)

        def load_first_batch(sp):
            sp.dma_start(x_sb[:, 0, 0:TT], tiles(x_mid[0])[0]).then_inc(ax_loaded, 16)

        assert GROUPS % 2 == 0 and BATCHES % 2 == 0
        ffn_phase(0, x_in, x_mid[0], 0, load_first_batch)
        attention_phase(x_mid[0], x_mid[1], GROUPS * NB)
        ffn_phase(1, x_mid[1], out, GROUPS * NB + BATCHES)


def kernel(**inputs):
    import numpy as _np
    import concourse.bacc as _bacc
    from concourse import mybir as _mybir
    from concourse.bass_utils import run_bass_kernel_spmd as _run

    x = _np.ascontiguousarray(inputs["L0_attn_hidden_states"])
    B, S, D = x.shape
    I = inputs["L0_ffn_w_gate"].shape[1]
    NR, J = 4, 128
    NCH, K = I // (NR * J), D // 128

    def members(w):
        return _np.asarray(w).reshape(K, 128, NCH, J, NR).transpose(2, 4, 1, 0, 3)

    def by_k(w):
        w = _np.asarray(w).T
        return _np.ascontiguousarray(w.reshape(K, 128, -1).transpose(1, 0, 2))

    HD = inputs["L0_attn_w_kv"].shape[0] // 2
    f = _np.float32
    even = _np.arange(0, HD, 2, dtype=f)
    inv = f(1.0) / _np.power(f(10000.0), even / f(HD)).astype(f)
    t = _np.arange(S, dtype=f)
    ang = _np.concatenate([t[:, None] * inv[None, :]] * 2, axis=-1).astype(f)
    base = (even + f(0.4 * HD)) / f(1.4 * HD)
    sc = _np.power(base[None, :], ((t - S // 2) / f(128))[:, None]).astype(f)
    sc = _np.concatenate([sc, sc], axis=-1)
    sign = _np.concatenate([-_np.ones(HD // 2, f), _np.ones(HD // 2, f)])
    tables = _np.stack([_np.cos(ang) * sc / f(HD), _np.sin(ang) * sc * sign / f(HD),
                        _np.cos(ang) / sc, _np.sin(ang) * sign / sc], axis=1).astype(f)
    tables = _np.ascontiguousarray(tables.reshape(S // 128, 128, 4, HD).transpose(1, 0, 2, 3))

    arrays = {
        "x": x,
        "w_gu": _np.ascontiguousarray(_np.stack([members(inputs["L0_ffn_w_gate"]), members(inputs["L0_ffn_w_up"])], axis=3)),
        "w_d": _np.ascontiguousarray(_np.asarray(inputs["L0_ffn_w_down"]).reshape(NCH, J, NR, D).transpose(0, 2, 1, 3)),
        "w_q": by_k(inputs["L0_attn_w_q"]),
        "w_kv": by_k(inputs["L0_attn_w_kv"]),
        "w_p": by_k(inputs["L0_attn_w_proj"]),
        "b_p": _np.ascontiguousarray(_np.asarray(inputs["L0_attn_b_proj"]).reshape(1, D)),
        "rotary": tables,
    }
    nc = _bacc.Bacc("TRN2", target_bir_lowering=False, num_devices=1)
    args = [nc.dram_tensor(f"in_{n}", a.shape, _mybir.dt.from_np(a.dtype), kind="ExternalInput").ap()
            for n, a in arrays.items()]
    args.append(nc.dram_tensor("out_0", x.shape, _mybir.dt.from_np(x.dtype), kind="ExternalOutput").ap())
    macaron_kernel(nc, *args)
    r = _run(nc, [{f"in_{n}": a for n, a in arrays.items()}], core_ids=[0])
    return r.results[0]["out_0"]
```
